# Optimizing a Trainium2 kernel written in Bass

```python
import numpy as np
import jax
import jax.numpy as jnp

def _softmax(x, axis=-1):
    return jax.nn.softmax(x, axis=axis)

def _gelu(x):
    return jax.nn.gelu(x, approximate=True)

def _silu(x):
    return jax.nn.silu(x)

def _sigmoid(x):
    return jax.nn.sigmoid(x)

def _layernorm(x, axis=-1, eps=1e-05):
    m = jnp.mean(x, axis=axis, keepdims=True)
    v = jnp.var(x, axis=axis, keepdims=True)
    return (x - m) / jnp.sqrt(v + eps)

def _scatter_add(tgt, idx, src, axis=0):
    return tgt.at[idx].add(src)

def _segment_sum(src, seg, n):
    return jax.ops.segment_sum(src, seg, n)
kernel_name = 'mk_vit_tower_cls_d1_tok_img768_r4_d9675c'

def setup_inputs(seed: int=0):
    np.random.seed(seed)
    _w = jnp.asarray

    def _rec_inputs():
        import jax
        import jax.numpy as jnp
        _rk = jax.random.key(seed)
        x = -0.00016672 + 0.999947 * jax.random.normal(jax.random.fold_in(_rk, 1), (128, 3, 64, 64), jnp.float32)
        cls_tok = 0.02 * jax.random.normal(jax.random.fold_in(_rk, 5), (1, 1, 192), jnp.float32)
        return (x, cls_tok)
    x, cls_tok = _rec_inputs()

    def _L0_tok_setup():
        import jax, jax.numpy as jnp
        import numpy as np
        BATCH = 64
        IN_CHANS = 3
        EMBED_DIM = 192
        IMG = 96
        OLD_PS = 32
        NEW_PS = 16

        def _compute_pinv(old_ps: int, new_ps: int) -> jnp.ndarray:
            old_hw = old_ps * old_ps
            basis = jnp.eye(old_hw, dtype=jnp.float32).reshape(old_hw, old_ps, old_ps)
            resize = lambda b: jax.image.resize(b, (new_ps, new_ps), method='cubic', antialias=True)
            resize_matrix = jax.vmap(resize)(basis).reshape(old_hw, new_ps * new_ps)
            return jnp.linalg.pinv(resize_matrix)
        key = jax.random.key(seed)
        k_x, k_w, k_b = jax.random.split(key, 3)
        x = jax.random.normal(k_x, (BATCH, IN_CHANS, IMG, IMG), dtype=jnp.float32)
        proj_weight = 0.02 * jax.random.normal(k_w, (EMBED_DIM, IN_CHANS, OLD_PS, OLD_PS), dtype=jnp.float32)
        proj_bias = 0.02 * jax.random.normal(k_b, (EMBED_DIM,), dtype=jnp.float32)
        pinv = _compute_pinv(OLD_PS, NEW_PS)
        return {'x': x, 'patch_size': NEW_PS, 'proj_weight': proj_weight, 'proj_bias': proj_bias, 'pinv': pinv}
    _L0_tok_all = _L0_tok_setup()
    _L0_tok_in = {k: v for k, v in _L0_tok_all.items() if k in ('proj_weight', 'proj_bias', 'pinv')}
    del _L0_tok_all

    def _L0_attn_setup():
        import jax, jax.numpy as jnp
        import numpy as np
        D_MODEL = 192
        N_HEADS = 12
        D_K = D_MODEL // N_HEADS
        key = jax.random.key(seed)
        k_x, k_wqkv, k_bqkv, k_wo, k_bo = jax.random.split(key, 5)
        s = 1.0 / np.sqrt(D_MODEL)
        return {'x': jax.random.normal(k_x, (2, 1024, D_MODEL), dtype=jnp.float32), 'w_qkv': jax.random.uniform(k_wqkv, (D_MODEL, 3 * D_MODEL), jnp.float32, -s, s), 'b_qkv': jax.random.uniform(k_bqkv, (3 * D_MODEL,), jnp.float32, -s, s), 'w_out': jax.random.uniform(k_wo, (D_MODEL, D_MODEL), jnp.float32, -s, s), 'b_out': jax.random.uniform(k_bo, (D_MODEL,), jnp.float32, -s, s)}
    _L0_attn_all = _L0_attn_setup()
    _L0_attn_in = {k: v for k, v in _L0_attn_all.items() if k in ('w_qkv', 'b_qkv', 'w_out', 'b_out')}
    del _L0_attn_all

    def _L0_ffn_setup():
        import jax, jax.numpy as jnp
        import numpy as np
        B, S, D_IN, D_HID, D_OUT = (32, 128, 192, 768, 192)
        key = jax.random.key(seed)
        k1, k2, k3, k4 = jax.random.split(key, 4)
        init_k = float(np.sqrt(1.0 / D_IN))
        init_k2 = float(np.sqrt(1.0 / D_HID))
        x = jax.random.normal(k1, (B, S, D_IN), dtype=jnp.float32)
        in_weight = jax.random.uniform(k2, (D_HID, D_IN), dtype=jnp.float32, minval=-init_k, maxval=init_k)
        in_bias = jax.random.uniform(k3, (D_HID,), dtype=jnp.float32, minval=-init_k, maxval=init_k)
        out_weight = jax.random.uniform(k4, (D_HID, D_OUT), dtype=jnp.float32, minval=-init_k2, maxval=init_k2)
        return {'x': x, 'in_weight': in_weight, 'in_bias': in_bias, 'out_weight': out_weight}
    _L0_ffn_all = _L0_ffn_setup()
    _L0_ffn_in = {k: v for k, v in _L0_ffn_all.items() if k in ('in_weight', 'in_bias', 'out_weight')}
    del _L0_ffn_all
    return {'x': x, 'cls_tok': cls_tok, 'L0_tok_proj_weight': _L0_tok_in['proj_weight'], 'L0_tok_proj_bias': _L0_tok_in['proj_bias'], 'L0_tok_pinv': _L0_tok_in['pinv'], 'L0_attn_w_qkv': _L0_attn_in['w_qkv'], 'L0_attn_b_qkv': _L0_attn_in['b_qkv'], 'L0_attn_w_out': _L0_attn_in['w_out'], 'L0_attn_b_out': _L0_attn_in['b_out'], 'L0_ffn_in_weight': _L0_ffn_in['in_weight'], 'L0_ffn_in_bias': _L0_ffn_in['in_bias'], 'L0_ffn_out_weight': _L0_ffn_in['out_weight']}

def reference(x, cls_tok, L0_tok_proj_weight, L0_tok_proj_bias, L0_tok_pinv, L0_attn_w_qkv, L0_attn_b_qkv, L0_attn_w_out, L0_attn_b_out, L0_ffn_in_weight, L0_ffn_in_bias, L0_ffn_out_weight):
    import jax
    import jax.numpy as jnp

    def _L0_tok_ref(x, patch_size, proj_weight, proj_bias, pinv):
        import jax, jax.numpy as jnp
        import numpy as np
        BATCH = 64
        IN_CHANS = 3
        EMBED_DIM = 192
        IMG = 96
        OLD_PS = 32
        NEW_PS = 16

        def _compute_pinv(old_ps: int, new_ps: int) -> jnp.ndarray:
            old_hw = old_ps * old_ps
            basis = jnp.eye(old_hw, dtype=jnp.float32).reshape(old_hw, old_ps, old_ps)
            resize = lambda b: jax.image.resize(b, (new_ps, new_ps), method='cubic', antialias=True)
            resize_matrix = jax.vmap(resize)(basis).reshape(old_hw, new_ps * new_ps)
            return jnp.linalg.pinv(resize_matrix)
        ps = int(patch_size)
        E, C, oh, ow = proj_weight.shape
        w = jnp.einsum('po,eco->ecp', pinv, proj_weight.reshape(E, C, oh * ow))
        w = w.reshape(E, C, ps, ps)
        B, _, H, W = x.shape
        gh, gw = (H // ps, W // ps)
        xp = x.reshape(B, C, gh, ps, gw, ps)
        out = jnp.einsum('bcipjq,ecpq->bije', xp, w) + proj_bias
        return out.reshape(B, gh * gw, E)

    def _L0_attn_ref(x, w_qkv, b_qkv, w_out, b_out):
        import jax, jax.numpy as jnp
        import numpy as np
        D_MODEL = 192
        N_HEADS = 12
        D_K = D_MODEL // N_HEADS
        B, S, E = x.shape
        qkv = x @ w_qkv + b_qkv
        qkv = qkv.reshape(B, S, 3, N_HEADS, D_K)
        qkv = jnp.transpose(qkv, (2, 0, 3, 1, 4))
        q, k, v = (qkv[0], qkv[1], qkv[2])
        scores = jnp.einsum('bhsd,bhtd->bhst', q, k) / jnp.sqrt(jnp.float32(D_K))
        attn = jax.nn.softmax(scores, axis=-1)
        ctx = jnp.einsum('bhst,bhtd->bhsd', attn, v)
        ctx = jnp.transpose(ctx, (0, 2, 1, 3)).reshape(B, S, E)
        return ctx @ w_out + b_out

    def _L0_ffn_ref(x, in_weight, in_bias, out_weight):
        import jax, jax.numpy as jnp
        import numpy as np
        B, S, D_IN, D_HID, D_OUT = (32, 128, 192, 768, 192)
        lead = x.shape[:-1]
        xt = x.reshape(-1, in_weight.shape[1])
        h = jax.nn.gelu(jnp.einsum('td,hd->th', xt, in_weight) + in_bias, approximate=False)
        out = jnp.einsum('th,ho->to', h, out_weight)
        return out.reshape(*lead, out_weight.shape[1])
    h = _L0_tok_ref(x, 16, L0_tok_proj_weight, L0_tok_proj_bias, L0_tok_pinv)
    h = jnp.concatenate([jnp.broadcast_to(cls_tok, (h.shape[0], 1, h.shape[2])), h], axis=1)
    h = h + _L0_attn_ref(_layernorm(h, axis=-1), L0_attn_w_qkv, L0_attn_b_qkv, L0_attn_w_out, L0_attn_b_out)
    h = h + _L0_ffn_ref(_layernorm(h, axis=-1), L0_ffn_in_weight, L0_ffn_in_bias, L0_ffn_out_weight)
    return h

_drawn_inputs = setup_inputs


def setup_inputs(seed=0):
    import zlib

    import numpy as np

    out = dict(_drawn_inputs(seed))
    spreads = {}
    factors = {'cls_tok': 2.965,
     'L0_tok_proj_bias': 3.901,
     'L0_attn_b_qkv': 2.921,
     'L0_ffn_in_bias': 5.034}
    for name, (base, spread) in spreads.items():
        noise = np.random.default_rng([zlib.crc32(name.encode()), seed]).standard_normal(out[name].shape)
        drawn = base * np.exp(spread * noise) if base else spread * noise
        out[name] = jnp.asarray(drawn.astype(out[name].dtype))
    for name, factor in factors.items():
        out[name] = (out[name] * factor).astype(out[name].dtype)
    return out
```

```python
from contextlib import ExitStack

import concourse.bass as bass
from concourse import mybir

F32 = mybir.dt.float32
ALU = mybir.AluOpType
ACT = mybir.ActivationFunctionType
AX = mybir.AxisListType

P = 128
E = 192
EH = E // 2
HEADS, DK = 12, 16
HH = HEADS // 2
B, C, PIX = 128, 3, 256
OLD = 1024
NP, NT = 16, 17
GB = 16
G = B // GB
GT = GB * NP
TILES = GT // P
QT = GB * NT
QW = QT + 32 - NT
SB = 8
STEPS = GB // SB
HK = HH * NT
HID = 768
HC = HID // P
XC = C * PIX // P
OC = OLD // P
EPS = 1e-5
SCALE = DK ** -0.5


def vit_tower(nc, xt, wt, pinvt, pbias, cls, wqkv, bqkv, wout, bout, win, bin_, w2, ident, hmask, out_p, out_c):
    with ExitStack() as ctx:
        def sb(name, shape, dt=F32):
            return ctx.enter_context(nc.sbuf_tensor(name, shape, dt))

        def pb(name):
            return ctx.enter_context(nc.psum_tensor(name, [P, 512], F32))

        def sem(name):
            return ctx.enter_context(nc.semaphore(name))

        wt_s = sb("wt_s", [P, OC, C * E])
        pinv_s = sb("pinv_s", [P, OC, PIX])
        wf = sb("wf", [P, 2, C, E])
        wqkv_s = sb("wqkv_s", [EH, 2, 3 * E])
        bqkv_s = sb("bqkv_s", [EH, 6])
        wout_s = sb("wout_s", [EH, 2, E])
        win_s = sb("win_s", [EH, 2, HID])
        bin_s = sb("bin_s", [P, HC])
        w2_s = sb("w2_s", [P, HC, E])
        pbias_s = sb("pbias_s", [P, E])
        bout_s = sb("bout_s", [P, E])
        id_s = sb("id_s", [P, P])
        mask_s = sb("mask_s", [EH, HH])
        mhalf = sb("mhalf", [P, TILES])
        x_s = sb("x_s", [P, 2, XC, GT])
        h_s = sb("h_s", [P, 2, TILES, E])
        hcls = sb("hcls", [P, E])
        hb_s = sb("hb_s", [P, 2, TILES, E])
        hbcls = sb("hbcls", [P, E])
        st = sb("st", [P, 2, TILES, 6])
        mv = sb("mv", [P, 2, TILES, 2])
        ve = sb("ve", [P, 2, TILES])
        rstd = sb("rstd", [P, 2, TILES])
        xn = sb("xn", [P, 2, TILES, E])
        xT1 = sb("xT1", [EH, 2, GT])
        xT2 = sb("xT2", [EH, 2, GT])
        qT = sb("qT", [EH, 2, 2, QW])
        kT = sb("kT", [EH, 2, 2, QT])
        vT = sb("vT", [EH, 2, 2, QT])
        kbd = sb("kbd", [EH, 2, 2, GB, HK])
        vm = sb("vm", [EH, 2, 2, GB, HK])
        vbd = sb("vbd", [HK, 2, 2, 2, 4, EH])
        ssub = sb("ssub", [P, 2, 2, HEADS * NT])
        pexp = sb("pexp", [P, 2, 2, HEADS * NT])
        smax = sb("smax", [P, 2, 2 * HEADS])
        ssum = sb("ssum", [P, 2, 2 * HEADS])
        rinv = sb("rinv", [P, 2, 2 * HEADS])
        pT = sb("pT", [HK, 2, 2, 2, P])
        cx = sb("cx", [P, 2, 2, E])
        cT = sb("cT", [EH, 2, 2, GT])
        cTc = sb("cTc", [EH, 2, B])
        h2 = sb("h2", [P, 2, TILES, E])
        h2c = sb("h2c", [P, E])
        gl = sb("gl", [P, HC, GT])
        os_ = sb("os", [P, 2, TILES, E])
        osc = sb("osc", [P, E])

        d_ps = [pb("d0"), pb("d1")]
        s_ps, pt_ps, pv_ps, ct_ps = pb("s_ps"), pb("pt_ps"), pb("pv_ps"), pb("ct_ps")
        v_ps = [pb("v0"), pb("v1")]
        fold_ps = [s_ps, pt_ps, v_ps[0], v_ps[1]]

        w_in = [sem(f"w_in{k}") for k in range(OC)]
        x_in = [sem("x_in0"), sem("x_in1")]
        cls_in, small_in, wqkv_in, late_in = sem("cls_in"), sem("small_in"), sem("wqkv_in"), sem("late_in")
        out_done = [sem("out_done0"), sem("out_done1"), sem("out_done2")]
        pe_fold, pe_embed, pe_t1, pe_qkv, pe_s, pe_pt, pe_vbd, pe_pv, pe_ct, pe_o, pe_t2, pe_f1, pe_f2 = map(sem, (
            "pe_fold", "pe_embed", "pe_t1", "pe_qkv", "pe_s", "pe_pt", "pe_vbd", "pe_pv", "pe_ct", "pe_o", "pe_t2",
            "pe_f1", "pe_f2"))
        pe_cls_t, pe_cls_qkv, pe_cls_o, pe_cls_t2, pe_cls_f1, pe_cls_f2 = map(sem, (
            "pe_cls_t", "pe_cls_qkv", "pe_cls_o", "pe_cls_t2", "pe_cls_f1", "pe_cls_f2"))
        act_x1, act_qkv, act_exp, act_pt, act_vbd, act_ct, act_x2, act_g = map(sem, (
            "act_x1", "act_qkv", "act_exp", "act_pt", "act_vbd", "act_ct", "act_x2", "act_g"))
        act_cls_x, act_cls_qkv, act_cls_x2, act_cls_g = map(sem, (
            "act_cls_x", "act_cls_qkv", "act_cls_x2", "act_cls_g"))
        dve_fold, dve_h, dve_xn, dve_k, dve_v, dve_sub, dve_cx, dve_h2, dve_xn2, dve_out, dve_ve, dve_chain = map(sem, (
            "dve_fold", "dve_h", "dve_xn", "dve_k", "dve_v", "dve_sub", "dve_cx", "dve_h2", "dve_xn2", "dve_out",
            "dve_ve", "dve_chain"))
        dve_cls_xn, dve_cls_h2, dve_cls_xn2, dve_cls_out, dve_init = map(sem, (
            "dve_cls_xn", "dve_cls_h2", "dve_cls_xn2", "dve_cls_out", "dve_init"))
        pool_rstd, pool_hb, pool_cls_hb = sem("pool_rstd"), sem("pool_hb"), sem("pool_cls_hb")

        order = [("cls", 0)]
        for i in range(-1, G + 1):
            if i + 1 < G:
                order.append(("ln1", i + 1))
            if i >= 1:
                order.append(("ln2", i - 1))
        order.append(("cls", 1))
        nth = {what: n + 1 for n, what in enumerate(order)}

        block = ctx.enter_context(nc.Block())

        @block.sync
        def _(sp):
            def load_x(g):
                if g >= 2:
                    sp.wait_ge(pe_embed, TILES * (g - 1))
                sp.dma_start(x_s[:, g % 2], xt[g]).then_inc(x_in[g % 2], 16)

            for k in range(OC):
                sp.dma_start(wt_s[:, k], wt[:, k]).then_inc(w_in[k], 16)
                if k % 2 == 0:
                    sp.dma_start(pinv_s[:, k:k + 2], pinvt[:, k:k + 2]).then_inc(w_in[k], 16)
            load_x(0)
            load_x(1)
            for dst, src in ((wout_s[:], wout), (win_s[:], win), (bin_s[:], bin_), (w2_s[:], w2)):
                sp.dma_start(dst, src).then_inc(late_in, 16)
            load_x(2)
            load_x(3)
            for g in range(G):
                if g + 4 < G:
                    load_x(g + 4)
                sp.wait_ge(dve_out, TILES * (g + 1))
                sp.dma_start(out_p[g], os_[:, g % 2]).then_inc(out_done[g % 2], 16)
            sp.wait_ge(dve_cls_out, 1)
            sp.dma_start(out_c, osc[:]).then_inc(out_done[2], 16)
            sp.wait_ge(out_done[0], 16 * (G // 2))
            sp.wait_ge(out_done[1], 16 * (G // 2))
            sp.wait_ge(out_done[2], 16)

        @block.tensor
        def _(pe):
            def mm(out, lhsT, rhs, start, stop):
                return pe.matmul(out, lhsT, rhs, start=start, stop=stop)

            def fold():
                for k in range(OC):
                    pe.wait_ge(w_in[k], 32 if k % 2 == 0 else 16)
                    if k % 2:
                        pe.wait_ge(w_in[k - 1], 32)
                    for ph in range(2):
                        for n in range(2):
                            last = mm(fold_ps[2 * ph + n][:, 0:288], pinv_s[:, k, ph * P:(ph + 1) * P],
                                      wt_s[:, k, n * 288:(n + 1) * 288], k == 0, k == OC - 1)
                            if k == OC - 1:
                                last.then_inc(pe_fold, 1)

            def embed(g, t):
                if t == 0:
                    pe.wait_ge(x_in[g % 2], 16 * (g // 2 + 1))
                for c in range(XC):
                    last = mm(d_ps[t][:, 0:E], x_s[:, g % 2, c, t * P:(t + 1) * P], wf[:, c % 2, c // 2, :],
                              c == 0, c == XC - 1)
                last.then_inc(pe_embed, 1)

            def transposes(bank, src, n):
                for t in range(n):
                    for hf in range(2):
                        last = pe.transpose(bank[0:EH, hf * n * P + t * P:hf * n * P + (t + 1) * P],
                                            src[:, t, hf * EH:(hf + 1) * EH], id_s[:, :])
                return last

            def project(bank, f, rhs, n, at=0):
                for m in range(2):
                    for kc in range(2):
                        last = mm(bank[0:EH, at + m * n:at + (m + 1) * n],
                                  wqkv_s[:, kc, f * E + m * EH:f * E + (m + 1) * EH], rhs[:, kc, 0:n],
                                  kc == 0, kc == 1)
                return last

            def scores(s):
                g = s // STEPS
                pe.wait_ge(dve_k, g + 1)
                if s >= 1:
                    pe.wait_ge(dve_sub, s)
                if s == 0:
                    pe.wait_ge(dve_fold, 4)
                for tl in range(2):
                    for j in range(4):
                        b = (s % STEPS) * SB + tl * 4 + j
                        for hf in range(2):
                            last = mm(s_ps[32 * j:32 * j + 32, tl * 204 + hf * HK:tl * 204 + (hf + 1) * HK],
                                      qT[:, g % 2, hf, b * NT:b * NT + 32],
                                      kbd[:, g % 2, hf, b, :], True, True)
                last.then_inc(pe_s, 1)

            def v_blocks(s, q):
                g, n = s // STEPS, 4 * s + q
                tl, hf = q // 2, q % 2
                if q == 0:
                    pe.wait_ge(dve_v, g + 1)
                if n >= 2:
                    pe.wait_ge(act_vbd, n - 1)
                for j in range(4):
                    b = (s % STEPS) * SB + tl * 4 + j
                    last = pe.transpose(v_ps[q % 2][0:HK, j * EH:(j + 1) * EH],
                                        vm[:, g % 2, hf, b, :], id_s[0:EH, 0:EH])
                last.then_inc(pe_vbd, 1)

            def p_transposes(s):
                pe.wait_ge(act_exp, s + 1)
                if s >= 1:
                    pe.wait_ge(act_pt, s)
                for tl in range(2):
                    for hf in range(2):
                        last = pe.transpose(pt_ps[0:HK, (tl * 2 + hf) * P:(tl * 2 + hf + 1) * P],
                                            pexp[:, s % 2, tl, hf * HK:(hf + 1) * HK], id_s[:, :])
                last.then_inc(pe_pt, 1)

            def pv(s):
                pe.wait_ge(act_pt, s + 1)
                pe.wait_ge(act_vbd, 4 * s + 4)
                if s >= 1:
                    pe.wait_ge(dve_cx, s)
                for tl in range(2):
                    for hf in range(2):
                        for j in range(4):
                            last = mm(pv_ps[32 * j:32 * j + 32, tl * E + hf * EH:tl * E + (hf + 1) * EH],
                                      pT[:, s % 2, tl, hf, 32 * j:32 * j + 32], vbd[:, s % 2, tl, hf, j, :],
                                      True, True)
                last.then_inc(pe_pv, 1)

            def c_transposes(s):
                pe.wait_ge(dve_cx, s + 1)
                if s >= 1:
                    pe.wait_ge(act_ct, s)
                for tl in range(2):
                    for hf in range(2):
                        last = pe.transpose(ct_ps[0:EH, (hf * 2 + tl) * P:(hf * 2 + tl + 1) * P],
                                            cx[:, s % 2, tl, hf * EH:(hf + 1) * EH], id_s[:, :])
                last.then_inc(pe_ct, 1)

            def out_proj(bank, lhs, n):
                for kc in range(2):
                    last = mm(bank[:, 0:E], lhs[:, kc, n * P:(n + 1) * P], wout_s[:, kc, :], kc == 0, kc == 1)
                return last

            def ffn1(bank, f, rhs, n):
                for m in range(2):
                    for kc in range(2):
                        last = mm(bank[:, m * n:(m + 1) * n], win_s[:, kc, (2 * f + m) * P:(2 * f + m + 1) * P],
                                  rhs[:, kc, 0:n], kc == 0, kc == 1)
                return last

            def ffn2(bank, t):
                for c in range(HC):
                    last = mm(bank[:, 0:E], gl[:, c, t * P:(t + 1) * P], w2_s[:, c, :], c == 0, c == HC - 1)
                return last

            fold()
            pe.wait_ge(small_in, 16 * 4)
            pe.wait_ge(dve_cls_xn, 1)
            transposes(d_ps[0], xn[:, 0], 1).then_inc(pe_cls_t, 1)
            pe.wait_ge(act_cls_x, 1)
            pe.wait_ge(wqkv_in, 32)
            for f in range(3):
                last = project(d_ps[1], f, xT1, GB, at=f * 2 * GB)
            last.then_inc(pe_cls_qkv, 1)
            pe.wait_ge(dve_fold, 4)
            pe.wait_ge(late_in, 16 * 4)

            for i in range(-1, G + 1):
                a, d = i + 1, i - 1
                att, emb, fin = 0 <= i < G, i + 1 < G, i >= 1
                s0 = STEPS * i
                if att:
                    scores(s0)
                    v_blocks(s0, 0)
                    v_blocks(s0, 1)
                if d >= 1:
                    pe.wait_ge(dve_out, TILES * d)
                if i == -1:
                    pe.wait_ge(act_cls_qkv, 1)
                if emb:
                    embed(a, 0)
                if att:
                    v_blocks(s0, 2)
                    v_blocks(s0, 3)
                if emb:
                    embed(a, 1)
                if att:
                    p_transposes(s0)
                if fin:
                    pe.wait_ge(act_ct, STEPS * (d + 1))
                    for t in range(TILES):
                        if emb:
                            pe.wait_ge(dve_h, TILES * a + t + 1)
                        out_proj(d_ps[t], cT[:, d % 2], t).then_inc(pe_o, 1)
                if att:
                    pv(s0)
                if emb:
                    pe.wait_ge(dve_xn, a + 1)
                    if fin:
                        pe.wait_ge(dve_h2, TILES * d + 1)
                    transposes(d_ps[0], xn[:, 0], TILES).then_inc(pe_t1, 1)
                if att:
                    c_transposes(s0)
                if emb:
                    pe.wait_ge(act_x1, a + 1)
                    if fin:
                        pe.wait_ge(dve_h2, TILES * d + 2)
                    project(d_ps[1], 0, xT1, GT).then_inc(pe_qkv, 1)
                    project(d_ps[0], 1, xT1, GT).then_inc(pe_qkv, 1)
                    pe.wait_ge(act_qkv, 3 * a + 1)
                    project(d_ps[1], 2, xT1, GT).then_inc(pe_qkv, 1)
                if fin:
                    pe.wait_ge(dve_xn2, d + 1)
                    if emb:
                        pe.wait_ge(act_qkv, 3 * a + 2)
                    transposes(d_ps[0], xn[:, 1], TILES).then_inc(pe_t2, 1)
                if att:
                    scores(s0 + 1)
                    v_blocks(s0 + 1, 0)
                    v_blocks(s0 + 1, 1)
                if fin:
                    pe.wait_ge(act_x2, d + 1)
                    if emb:
                        pe.wait_ge(act_qkv, 3 * a + 3)
                    ffn1(d_ps[1], 0, xT2, GT).then_inc(pe_f1, 1)
                if att:
                    v_blocks(s0 + 1, 2)
                    v_blocks(s0 + 1, 3)
                if fin:
                    ffn1(d_ps[0], 1, xT2, GT).then_inc(pe_f1, 1)
                if att:
                    p_transposes(s0 + 1)
                if fin:
                    pe.wait_ge(act_g, 3 * d + 1)
                    ffn1(d_ps[1], 2, xT2, GT).then_inc(pe_f1, 1)
                if att:
                    pv(s0 + 1)
                if fin:
                    pe.wait_ge(act_g, 3 * d + 3)
                    ffn2(d_ps[0], 0).then_inc(pe_f2, 1)
                if att:
                    c_transposes(s0 + 1)
                if fin:
                    ffn2(d_ps[1], 1).then_inc(pe_f2, 1)

            pe.wait_ge(dve_out, TILES * G)
            out_proj(d_ps[0], cTc, 0).then_inc(pe_cls_o, 1)
            pe.wait_ge(dve_cls_xn2, 1)
            transposes(d_ps[1], xn[:, 1], 1).then_inc(pe_cls_t2, 1)
            pe.wait_ge(act_cls_x2, 1)
            ffn1(d_ps[0], 0, xT2, P)
            ffn1(d_ps[1], 1, xT2, P)
            ffn1(v_ps[0], 2, xT2, P).then_inc(pe_cls_f1, 1)
            pe.wait_ge(act_cls_g, 1)
            ffn2(d_ps[0], 0).then_inc(pe_cls_f2, 1)

        @block.scalar
        def _(act):
            for dst, src in ((hcls[:], cls.partition_broadcast(P)),):
                act.dma_start(dst, src).then_inc(cls_in, 16)
            for dst, src in ((id_s[:], ident), (mask_s[:], hmask), (pbias_s[:], pbias.partition_broadcast(P)),
                             (bout_s[:], bout.partition_broadcast(P))):
                act.dma_start(dst, src).then_inc(small_in, 16)
            for dst, src in ((wqkv_s[:], wqkv), (bqkv_s[:], bqkv)):
                act.dma_start(dst, src).then_inc(wqkv_in, 16)

            def exp(s):
                act.wait_ge(dve_sub, s + 1)
                if s >= 2:
                    act.wait_ge(pe_pt, s - 1)
                act.activation(pexp[:, s % 2], ssub[:, s % 2], ACT.Exp, scale=SCALE).then_inc(act_exp, 1)

            def p_out(s):
                act.wait_ge(pe_pt, s + 1)
                if s >= 2:
                    act.wait_ge(pe_pv, s - 1)
                act.activation(pT[:, s % 2].rearrange("p a b q -> p (a b q)"), pt_ps[0:HK, :],
                               ACT.Copy).then_inc(act_pt, 1)

            def v_out(s, q):
                n = 4 * s + q
                act.wait_ge(pe_vbd, n + 1)
                if q == 0 and s >= 2:
                    act.wait_ge(pe_pv, s - 1)
                act.activation(vbd[:, s % 2, q // 2, q % 2].rearrange("p j e -> p (j e)"),
                               v_ps[q % 2][0:HK, 0:4 * EH], ACT.Copy).then_inc(act_vbd, 1)

            def c_out(s):
                g = s // STEPS
                act.wait_ge(pe_ct, s + 1)
                if s % STEPS == 0 and g >= 2:
                    act.wait_ge(pe_o, TILES * (g - 1))
                src = ct_ps[0:EH, :].rearrange("p (h b q) -> p h b q", h=2, q=32)
                dst = cT[:, g % 2, :, (s % STEPS) * P:(s % STEPS + 1) * P].rearrange("p h (b q) -> p h b q", q=NP)
                act.activation(dst, src[:, :, :, 0:NP], ACT.Copy)
                act.activation(cTc[:, :, s * SB:(s + 1) * SB], src[:, :, :, NP], ACT.Copy).then_inc(act_ct, 1)

            def with_bias(f, m, src, dst):
                return act.activation(dst, src, ACT.Identity, bias=bqkv_s[:, 2 * f + m:2 * f + m + 1])

            def qkv_out(g, f):
                act.wait_ge(pe_qkv, 3 * g + f + 1)
                if g >= 2:
                    if f == 0:
                        act.wait_ge(pe_s, STEPS * (g - 1))
                    else:
                        act.wait_ge((dve_k, dve_v)[f - 1], g - 1)
                for m in range(2):
                    dst = (qT, kT, vT)[f][:, g % 2, m, 0:QT].rearrange("p (b t) -> p b t", t=NT)[:, :, 0:NP]
                    src = d_ps[f % 2 == 0][0:EH, m * GT:(m + 1) * GT].rearrange("p (b t) -> p b t", t=NP)
                    last = with_bias(f, m, src, dst)
                last.then_inc(act_qkv, 1)

            def turn_out(bank, dst, n):
                return act.activation(dst[:, :, 0:n], bank[0:EH, 0:2 * n].rearrange("p (h t) -> p h t", h=2), ACT.Copy)

            def gelu(g, f):
                act.wait_ge(pe_f1, 3 * g + f + 1)
                if f == 0 and g >= 1:
                    act.wait_ge(pe_f2, TILES * g)
                for m in range(2):
                    last = act.activation(gl[:, 2 * f + m, :], d_ps[f % 2 == 0][:, m * GT:(m + 1) * GT], ACT.Gelu,
                                          bias=bin_s[:, 2 * f + m:2 * f + m + 1])
                last.then_inc(act_g, 1)

            act.wait_ge(pe_cls_t, 1)
            turn_out(d_ps[0], xT1, P).then_inc(act_cls_x, 1)
            act.wait_ge(wqkv_in, 32)
            act.wait_ge(pe_cls_qkv, 1)
            act.wait_ge(dve_init, 1)
            for f in range(3):
                for m in range(2):
                    for r in range(2):
                        dst = (qT, kT, vT)[f][:, r, m, 0:QT].rearrange("p (b t) -> p b t", t=NT)[:, :, NP]
                        last = with_bias(f, m, d_ps[1][0:EH, (2 * f + m) * GB:(2 * f + m + 1) * GB], dst)
            last.then_inc(act_cls_qkv, 1)

            for i in range(-1, G + 1):
                a, d = i + 1, i - 1
                att, emb, fin = 0 <= i < G, i + 1 < G, i >= 1
                s0 = STEPS * i
                if att:
                    v_out(s0, 0)
                    v_out(s0, 1)
                    exp(s0)
                    v_out(s0, 2)
                    v_out(s0, 3)
                    p_out(s0)
                if emb:
                    act.wait_ge(pe_t1, a + 1)
                    if a >= 1:
                        act.wait_ge(pe_qkv, 3 * a)
                    turn_out(d_ps[0], xT1, GT).then_inc(act_x1, 1)
                if att:
                    c_out(s0)
                if emb:
                    for f in range(3):
                        qkv_out(a, f)
                if fin:
                    act.wait_ge(pe_t2, d + 1)
                    if d >= 1:
                        act.wait_ge(pe_f1, 3 * d)
                    turn_out(d_ps[0], xT2, GT).then_inc(act_x2, 1)
                if att:
                    v_out(s0 + 1, 0)
                    v_out(s0 + 1, 1)
                    exp(s0 + 1)
                    v_out(s0 + 1, 2)
                    v_out(s0 + 1, 3)
                if fin:
                    gelu(d, 0)
                    gelu(d, 1)
                if att:
                    p_out(s0 + 1)
                if fin:
                    gelu(d, 2)
                if att:
                    c_out(s0 + 1)

            act.wait_ge(pe_cls_t2, 1)
            act.wait_ge(pe_f1, 3 * G)
            turn_out(d_ps[1], xT2, P).then_inc(act_cls_x2, 1)
            act.wait_ge(pe_cls_f1, 1)
            act.wait_ge(pe_f2, TILES * G)
            for c in range(HC):
                bank = (d_ps[0], d_ps[1], v_ps[0])[c // 2]
                last = act.activation(gl[:, c, 0:P], bank[:, (c % 2) * P:(c % 2 + 1) * P], ACT.Gelu,
                                      bias=bin_s[:, c:c + 1])
            last.then_inc(act_cls_g, 1)

        @block.vector
        def _(dve):
            linked = [0]

            def link(ins):
                linked[0] += 1
                ins.then_inc(dve_chain, 1)
                dve.wait_ge(dve_chain, linked[0])

            def stats(src, ln, n):
                for t in range(n):
                    link(dve.bn_stats(st[:, ln, t, :], src[:, t, :]))
                for t in range(n):
                    ins = dve.bn_aggr(mv[:, ln, t, :], st[:, ln, t, :])
                link(ins)
                dve.tensor_scalar(ve[:, ln, 0:n], mv[:, ln, 0:n, 1], EPS, None, ALU.add).then_inc(dve_ve, 1)

            def normalise(src, ln, n, what):
                dve.wait_ge(pool_rstd, nth[what])
                for t in range(n):
                    ins = dve.tensor_scalar(xn[:, ln, t, :], src[:, t, :], mv[:, ln, t, 0:1], rstd[:, ln, t:t + 1],
                                            ALU.subtract, ALU.mult)
                return ins

            def softmax_top(s):
                dve.wait_ge(pe_s, s + 1)
                sc = s_ps[:, 0:2 * HEADS * NT].rearrange("p (h k) -> p h k", k=NT)
                link(dve.tensor_reduce(smax[:, s % 2], sc, AX.X, ALU.max))
                if s >= 2:
                    dve.wait_ge(act_exp, s - 1)
                dve.tensor_tensor(ssub[:, s % 2].rearrange("p a (h k) -> p (a h) k", k=NT), sc,
                                  smax[:, s % 2].unsqueeze(2).to_broadcast([P, 2 * HEADS, NT]),
                                  ALU.subtract).then_inc(dve_sub, 1)

            def softmax_sum(s):
                dve.wait_ge(act_exp, s + 1)
                link(dve.tensor_reduce(ssum[:, s % 2], pexp[:, s % 2].rearrange("p a (h k) -> p (a h) k", k=NT),
                                       AX.X, ALU.add))
                dve.reciprocal(rinv[:, s % 2], ssum[:, s % 2]).then_inc(dve_chain, 1)
                linked[0] += 1
                return linked[0]

            def context(s, summed):
                dve.wait_ge(pe_pv, s + 1)
                dve.wait_ge(dve_chain, summed)
                if s >= 2:
                    dve.wait_ge(pe_ct, s - 1)
                dve.tensor_tensor(cx[:, s % 2].rearrange("p a (h d) -> p (a h) d", d=DK),
                                  pv_ps[:, 0:2 * E].rearrange("p (h d) -> p h d", d=DK),
                                  rinv[:, s % 2].unsqueeze(2).to_broadcast([P, 2 * HEADS, DK]),
                                  ALU.mult).then_inc(dve_cx, 1)

            def masks(g, src, dst, f, done):
                dve.wait_ge(act_qkv, 3 * g + f + 1)
                if g >= 2:
                    if f == 1:
                        dve.wait_ge(pe_s, STEPS * (g - 1))
                    else:
                        dve.wait_ge(pe_vbd, 4 * STEPS * (g - 1))
                for h in range(HH):
                    ins = dve.tensor_scalar(
                        dst[:, g % 2, :, :, h * NT:(h + 1) * NT].rearrange("p a b t -> p (a b) t"),
                        src[:, g % 2].rearrange("p a (b t) -> p (a b) t", t=NT), mask_s[:, h:h + 1], None, ALU.mult)
                ins.then_inc(done, 1)

            dve.memset(mhalf[:], -0.5)
            for r in range(2):
                for m in range(2):
                    ins = dve.memset(qT[:, r, m, QT:QW], 0.0)
            ins.then_inc(dve_init, 1)
            dve.wait_ge(cls_in, 16)
            stats(hcls[:].unsqueeze(1), 0, 1)
            normalise(hcls[:].unsqueeze(1), 0, 1, ("cls", 0)).then_inc(dve_cls_xn, 1)
            for n in range(4):
                dve.wait_ge(pe_fold, n + 1)
                dve.tensor_copy(wf[:, n // 2].rearrange("p c e -> p (c e)")[:, (n % 2) * 288:(n % 2 + 1) * 288],
                                fold_ps[n][:, 0:288]).then_inc(dve_fold, 1)
            dve.wait_ge(small_in, 16 * 4)

            for i in range(-1, G + 1):
                a, d = i + 1, i - 1
                att, emb, fin = 0 <= i < G, i + 1 < G, i >= 1
                s0 = STEPS * i
                if att:
                    softmax_top(s0)
                if emb:
                    for t in range(TILES):
                        dve.wait_ge(pe_embed, TILES * a + t + 1)
                        if a >= 2 and t == 0:
                            dve.wait_ge(pool_hb, a - 1)
                        ins = dve.tensor_tensor(h_s[:, a % 2, t, :], d_ps[t][:, 0:E], pbias_s[:], ALU.add)
                        ins.then_inc(dve_h, 1)
                    dve.wait_ge(dve_h, TILES * (a + 1))
                    stats(h_s[:, a % 2], 0, TILES)
                if att:
                    summed = softmax_sum(s0)
                if fin:
                    dve.wait_ge(pool_hb, d + 1)
                    for t in range(TILES):
                        dve.wait_ge(pe_o, TILES * d + t + 1)
                        dve.tensor_tensor(h2[:, d % 2, t, :], d_ps[t][:, 0:E], hb_s[:, d % 2, t, :],
                                          ALU.add).then_inc(dve_h2, 1)
                if emb:
                    if a >= 1:
                        dve.wait_ge(pe_t1, a)
                    else:
                        dve.wait_ge(pe_cls_t, 1)
                    normalise(h_s[:, a % 2], 0, TILES, ("ln1", a)).then_inc(dve_xn, 1)
                if fin:
                    dve.wait_ge(dve_h2, TILES * (d + 1))
                    stats(h2[:, d % 2], 1, TILES)
                if att:
                    context(s0, summed)
                if fin:
                    if d >= 1:
                        dve.wait_ge(pe_t2, d)
                    normalise(h2[:, d % 2], 1, TILES, ("ln2", d)).then_inc(dve_xn2, 1)
                if emb:
                    if i == -1:
                        dve.wait_ge(act_cls_qkv, 1)
                    masks(a, kT, kbd, 1, dve_k)
                if att:
                    softmax_top(s0 + 1)
                    summed = softmax_sum(s0 + 1)
                if emb:
                    masks(a, vT, vm, 2, dve_v)
                if att:
                    context(s0 + 1, summed)
                if fin:
                    if d >= 2:
                        dve.wait_ge(out_done[d % 2], 16 * (d // 2))
                    for t in range(TILES):
                        dve.wait_ge(pe_f2, TILES * d + t + 1)
                        dve.tensor_tensor(os_[:, d % 2, t, :], d_ps[t][:, 0:E], h2[:, d % 2, t, :],
                                          ALU.add).then_inc(dve_out, 1)

            dve.wait_ge(pe_cls_o, 1)
            dve.wait_ge(pool_cls_hb, 1)
            dve.tensor_tensor(h2c[:], d_ps[0][:, 0:E], hbcls[:], ALU.add).then_inc(dve_cls_h2, 1)
            dve.wait_ge(dve_cls_h2, 1)
            stats(h2c[:].unsqueeze(1), 1, 1)
            dve.wait_ge(pe_t2, G)
            normalise(h2c[:].unsqueeze(1), 1, 1, ("cls", 1)).then_inc(dve_cls_xn2, 1)
            dve.wait_ge(pe_cls_f2, 1)
            dve.tensor_tensor(osc[:], d_ps[0][:, 0:E], h2c[:], ALU.add).then_inc(dve_cls_out, 1)

        @block.gpsimd
        def _(pool):
            def inverse_root(ln, n, what):
                pool.wait_ge(dve_ve, nth[what])
                pool.tensor_tensor(rstd[:, ln, 0:n], ve[:, ln, 0:n], mhalf[:, 0:n], ALU.pow).then_inc(pool_rstd, 1)

            pool.wait_ge(dve_init, 1)
            inverse_root(0, 1, ("cls", 0))
            pool.wait_ge(small_in, 16 * 4)
            pool.wait_ge(cls_in, 16)
            pool.tensor_tensor(hbcls[:], hcls[:], bout_s[:], ALU.add).then_inc(pool_cls_hb, 1)
            for i in range(-1, G + 1):
                a, d = i + 1, i - 1
                if a < G:
                    inverse_root(0, TILES, ("ln1", a))
                if d >= 0:
                    inverse_root(1, TILES, ("ln2", d))
                if a < G:
                    if a >= 2:
                        pool.wait_ge(dve_h2, TILES * (a - 1))
                    for t in range(TILES):
                        ins = pool.tensor_tensor(hb_s[:, a % 2, t, :], h_s[:, a % 2, t, :], bout_s[:], ALU.add)
                    ins.then_inc(pool_hb, 1)
            inverse_root(1, 1, ("cls", 1))


def kernel(x, cls_tok, L0_tok_proj_weight, L0_tok_proj_bias, L0_tok_pinv, L0_attn_w_qkv, L0_attn_b_qkv,
           L0_attn_w_out, L0_attn_b_out, L0_ffn_in_weight, L0_ffn_in_bias, L0_ffn_out_weight):
    import numpy as np
    import concourse.bacc as bacc
    from concourse.bass_utils import run_bass_kernel_spmd

    def lay(a):
        return np.ascontiguousarray(a)

    xp = np.asarray(x).reshape(G, GB, C, 4, 16, 4, 16).transpose(0, 2, 4, 6, 1, 3, 5)
    xp = xp.reshape(G, XC, P, GT).transpose(0, 2, 1, 3)
    wt = np.asarray(L0_tok_proj_weight).reshape(E, C, OC, P).transpose(3, 2, 1, 0).reshape(P, OC, C * E)
    pinvt = np.asarray(L0_tok_pinv).reshape(PIX, OC, P).transpose(2, 1, 0)
    arrays = {
        "xt": lay(xp), "wt": lay(wt), "pinvt": lay(pinvt),
        "pbias": lay(L0_tok_proj_bias), "cls": lay(np.asarray(cls_tok).reshape(E)),
        "wqkv": lay(np.asarray(L0_attn_w_qkv).reshape(2, EH, 3 * E).transpose(1, 0, 2)),
        "bqkv": lay(np.asarray(L0_attn_b_qkv).reshape(6, EH).T),
        "wout": lay(np.asarray(L0_attn_w_out).reshape(2, EH, E).transpose(1, 0, 2)),
        "bout": lay(L0_attn_b_out),
        "win": lay(np.asarray(L0_ffn_in_weight).T.reshape(2, EH, HID).transpose(1, 0, 2)),
        "bin_": lay(np.asarray(L0_ffn_in_bias).reshape(HC, P).T),
        "w2": lay(np.asarray(L0_ffn_out_weight).reshape(HC, P, E).transpose(1, 0, 2)),
        "ident": np.eye(P, dtype=np.float32),
        "hmask": np.repeat(np.eye(HH, dtype=np.float32), DK, axis=0),
    }
    nc = bacc.Bacc("TRN2", target_bir_lowering=False, num_devices=1)
    args = [nc.dram_tensor(n, a.shape, F32, kind="ExternalInput").ap() for n, a in arrays.items()]
    out_p = nc.dram_tensor("out_p", [G, P, TILES, E], F32, kind="ExternalOutput").ap()
    out_c = nc.dram_tensor("out_c", [B, E], F32, kind="ExternalOutput").ap()
    vit_tower(nc, *args, out_p, out_c)
    r = run_bass_kernel_spmd(nc, [arrays], core_ids=[0]).results[0]
    patches = np.asarray(r["out_p"]).transpose(0, 2, 1, 3).reshape(B, NP, E)
    return np.concatenate([np.asarray(r["out_c"]).reshape(B, 1, E), patches], axis=1)
```

```python
from contextlib import ExitStack

import concourse.bass as bass
from concourse import mybir

F32 = mybir.dt.float32
F32R = mybir.dt.float32r
ALU = mybir.AluOpType
ACT = mybir.ActivationFunctionType
AX = mybir.AxisListType

P = 128
E = 192
EH = E // 2
HEADS, DK = 12, 16
HH = HEADS // 2
B, C, PIX = 128, 3, 256
OLD = 1024
NP, NT = 16, 17
GB = 16
G = B // GB
GT = GB * NP
TILES = GT // P
QT = GB * NT
QW = QT + 32 - NT
SB = 8
STEPS = GB // SB
HK = HH * NT
HID = 768
HC = HID // P
XC = C * PIX // P
OC = OLD // P
EPS = 1e-5
SCALE = DK ** -0.5


def vit_tower(nc, xt, wt, pinvt, pbias, cls, wqkv, bqkv, wout, bout, win, bin_, w2, ident, hmask, out_p, out_c):
    with ExitStack() as ctx:
        def sb(name, shape, dt=F32):
            return ctx.enter_context(nc.sbuf_tensor(name, shape, dt))

        def pb(name):
            return ctx.enter_context(nc.psum_tensor(name, [P, 512], F32))

        def sem(name):
            return ctx.enter_context(nc.semaphore(name))

        wt_s = sb("wt_s", [P, OC, C * E])
        pinv_s = sb("pinv_s", [P, OC, PIX])
        wf = sb("wf", [P, 2, C, E])
        wqkv_raw = sb("wqkv_raw", [P, 3, 3 * E])
        wqkv_hi = sb("wqkv_hi", [P, 3, 3 * E], F32R)
        wqkv_lo = sb("wqkv_lo", [P, 2, 3 * E], F32R)
        win_hi = sb("win_hi", [P, 3, HID], F32R)
        win_lo = sb("win_lo", [P, 2, HID], F32R)
        bqkv_s = sb("bqkv_s", [EH, 6])
        wout_s = sb("wout_s", [EH, 2, E])
        bin_s = sb("bin_s", [P, HC])
        w2_s = sb("w2_s", [P, HC, E])
        pbias_s = sb("pbias_s", [P, E])
        bout_s = sb("bout_s", [P, E])
        id_s = sb("id_s", [P, P])
        id_r = sb("id_r", [P, P], F32R)
        mask_s = sb("mask_s", [EH, HH])
        mhalf = sb("mhalf", [P, TILES + 1])
        x_s = sb("x_s", [P, 2, XC, GT])
        h_s = sb("h_s", [P, TILES, E])
        hcls = sb("hcls", [P, E])
        hb_s = sb("hb_s", [P, G, TILES, E])
        hbcls = sb("hbcls", [P, E])
        st = sb("st", [P, 2, TILES + 1, 6])
        mv = sb("mv", [P, 2, TILES + 1, 2])
        ve = sb("ve", [P, 2, TILES + 1])
        rstd = sb("rstd", [P, 2, TILES + 1])
        xn1 = sb("xn1", [P, TILES, E])
        xn2 = sb("xn2", [P, TILES + 1, E])
        xs1 = sb("xs1", [P, TILES, 2, E], F32R)
        xs2 = sb("xs2", [P, TILES + 1, 2, E], F32R)
        xT1 = sb("xT1", [P, 3, GT], F32R)
        xT2 = sb("xT2", [P, 3, GT + P], F32R)
        qT = sb("qT", [EH, 2, 2, QW])
        kT = sb("kT", [EH, 2, QT])
        vT = sb("vT", [EH, 2, QT])
        kbd = sb("kbd", [EH, 2, 2, GB, HK])
        vm = sb("vm", [EH, 2, 2, GB, HK])
        vbd = sb("vbd", [HK, 2, 2, 4, EH])
        ssub = sb("ssub", [P, 2, HEADS * NT])
        pexp = sb("pexp", [P, 2, HEADS * NT])
        smax = sb("smax", [P, 2 * HEADS])
        ssum = sb("ssum", [P, 2 * HEADS])
        rinv = sb("rinv", [P, 2 * HEADS])
        pT = sb("pT", [HK, 2, 2, P])
        cx = sb("cx", [P, 2, E])
        cT = sb("cT", [EH, 2, 2, GT])
        cTc = sb("cTc", [EH, 2, B])
        h2 = sb("h2", [P, 2, TILES, E])
        h2c = sb("h2c", [P, E])
        win_raw = wt_s[:, 0:4, :].rearrange("p a b -> p (a b)").rearrange("p (c h) -> p c h", c=3)
        gl = wt_s[:, 4:8, :].rearrange("p a b -> p (a b)").rearrange("p (c h) -> p c h", c=HC)
        os_ = sb("os", [P, 2, TILES, E])
        osc = sb("osc", [P, E])

        d_ps = [pb("d0"), pb("d1"), pb("d2"), pb("d3")]
        s_ps, a_ps = pb("s_ps"), pb("a_ps")
        v_ps = [pb("v0"), pb("v1")]
        fold_ps = [s_ps, a_ps, v_ps[0], v_ps[1]]

        def qkv_bank(p, f):
            return d_ps[(2, 3, 0 if p else 1)[f]]

        def turn_bank(p, t):
            return d_ps[t + (2 if p else 0)]

        def ffn_bank(g, f):
            return d_ps[(3, 2 if g == G - 2 else 0, 1)[f]]

        w_in = [sem(f"w_in{k}") for k in range(OC)]
        x_in = [sem("x_in0"), sem("x_in1")]
        cls_in, small_in, wqkv_in, late_in, win_in = map(sem, ("cls_in", "small_in", "wqkv_in", "late_in", "win_in"))
        out_done = [sem("out_done0"), sem("out_done1"), sem("out_done2")]
        pe_fold, pe_embed, pe_t1, pe_qkv, pe_s, pe_pt, pe_vbd, pe_pv, pe_ct, pe_o, pe_t2, pe_f1, pe_f2 = map(sem, (
            "pe_fold", "pe_embed", "pe_t1", "pe_qkv", "pe_s", "pe_pt", "pe_vbd", "pe_pv", "pe_ct", "pe_o", "pe_t2",
            "pe_f1", "pe_f2"))
        pe_cls_t, pe_cls_qkv = sem("pe_cls_t"), sem("pe_cls_qkv")
        act_x1, act_qkv, act_exp, act_pt, act_vbd, act_ct, act_x2, act_g, act_hi1, act_hi2, act_w = map(sem, (
            "act_x1", "act_qkv", "act_exp", "act_pt", "act_vbd", "act_ct", "act_x2", "act_g", "act_hi1", "act_hi2",
            "act_w"))
        act_cls_x, act_cls_hi, act_cls_qkv = map(sem, ("act_cls_x", "act_cls_hi", "act_cls_qkv"))
        dve_fold, dve_h, dve_xn, dve_lo, dve_k, dve_v, dve_sub, dve_cx, dve_h2, dve_xn2, dve_lo2, dve_out = map(sem, (
            "dve_fold", "dve_h", "dve_xn", "dve_lo", "dve_k", "dve_v", "dve_sub", "dve_cx", "dve_h2", "dve_xn2",
            "dve_lo2", "dve_out"))
        dve_ve, dve_chain, dve_cls_xn, dve_cls_lo, dve_init, dve_w = map(sem, (
            "dve_ve", "dve_chain", "dve_cls_xn", "dve_cls_lo", "dve_init", "dve_w"))
        pool_rstd, pool_hb = sem("pool_rstd"), sem("pool_hb")

        ITER = range(-2, G + 1)

        order = [("cls", 0)]
        for i in ITER:
            if i >= 1:
                order.append(("ln2", i - 1))
            if i == G - 1:
                order.append(("early", 0))
            if i + 2 < G:
                order.append(("ln1", i + 2))
        nth = {what: n + 1 for n, what in enumerate(order)}

        block = ctx.enter_context(nc.Block())

        @block.sync
        def _(sp):
            def load_x(g):
                if g >= 2:
                    sp.wait_ge(pe_embed, TILES * (g - 1))
                sp.dma_start(x_s[:, g % 2], xt[g]).then_inc(x_in[g % 2], 16)

            for k in range(OC):
                sp.dma_start(wt_s[:, k], wt[:, k]).then_inc(w_in[k], 16)
                if k % 2 == 0:
                    sp.dma_start(pinv_s[:, k:k + 2], pinvt[:, k:k + 2]).then_inc(w_in[k], 16)
            load_x(0)
            load_x(1)
            load_x(2)
            sp.wait_ge(pe_fold, 4)
            sp.dma_start(win_raw, win).then_inc(win_in, 16)
            for dst, src in ((wout_s[:], wout), (bin_s[:], bin_), (w2_s[:], w2)):
                sp.dma_start(dst, src).then_inc(late_in, 16)
            load_x(3)
            load_x(4)
            for g in range(G):
                if g + 5 < G:
                    load_x(g + 5)
                sp.wait_ge(dve_out, TILES * (g + 1))
                sp.dma_start(out_p[g], os_[:, g % 2]).then_inc(out_done[g % 2], 16)
            sp.wait_ge(dve_out, TILES * G + 1)
            sp.dma_start(out_c, osc[:]).then_inc(out_done[2], 16)
            sp.wait_ge(out_done[0], 16 * (G // 2))
            sp.wait_ge(out_done[1], 16 * (G // 2))
            sp.wait_ge(out_done[2], 16)

        @block.tensor
        def _(pe):
            def mm(out, lhsT, rhs, start, stop):
                return pe.matmul(out, lhsT, rhs, start=start, stop=stop)

            def split_product(out, hi, lo, cols, xT, n):
                mm(out, hi[:, 0, cols], xT[:, 0, 0:n], True, False)
                mm(out, lo[:, 0, cols], xT[:, 0, 0:n], False, False)
                mm(out, lo[0:E - P, 1, cols], xT[0:E - P, 1, 0:n], False, False)
                mm(out, hi[:, 1, cols], xT[:, 1, 0:n], False, False)
                return mm(out, hi[:, 2, cols], xT[:, 2, 0:n], False, True)

            def fold(k):
                pe.wait_ge(w_in[k], 32 if k % 2 == 0 else 16)
                for ph in range(2):
                    for n in range(2):
                        last = mm(fold_ps[2 * ph + n][:, 0:288], pinv_s[:, k, ph * P:(ph + 1) * P],
                                  wt_s[:, k, n * 288:(n + 1) * 288], k == 0, k == OC - 1)
                        if k == OC - 1:
                            last.then_inc(pe_fold, 1)

            def embed(g, t, bank):
                if t == 0:
                    pe.wait_ge(x_in[g % 2], 16 * (g // 2 + 1))
                for c in range(XC):
                    last = mm(bank[:, 0:E], x_s[:, g % 2, c, t * P:(t + 1) * P], wf[:, c % 2, c // 2, :],
                              c == 0, c == XC - 1)
                last.then_inc(pe_embed, 1)

            def turn(bank, xs, t):
                src = xs[:, t].rearrange("p a e -> p (a e)")
                for c in range(3):
                    last = pe.transpose(bank[:, c * P:(c + 1) * P].bitcast(F32R), src[:, c * P:(c + 1) * P], id_r[:, :])
                return last

            def project(bank, f, n, at=0):
                for m in range(2):
                    last = split_product(bank[0:EH, at + m * n:at + (m + 1) * n], wqkv_hi, wqkv_lo,
                                         slice(f * E + m * EH, f * E + (m + 1) * EH), xT1, n)
                return last

            def scores(s):
                g = s // STEPS
                pe.wait_ge(dve_k, g + 1)
                if s >= 1:
                    pe.wait_ge(dve_sub, s)
                for tl in range(2):
                    for j in range(4):
                        b = (s % STEPS) * SB + tl * 4 + j
                        for hf in range(2):
                            last = mm(s_ps[32 * j:32 * j + 32, tl * 204 + hf * HK:tl * 204 + (hf + 1) * HK],
                                      qT[:, g % 2, hf, b * NT:b * NT + 32], kbd[:, g % 2, hf, b, :], True, True)
                last.then_inc(pe_s, 1)

            def v_blocks(s, q):
                g, n = s // STEPS, 4 * s + q
                tl, hf = q // 2, q % 2
                if q == 0:
                    pe.wait_ge(dve_v, g + 1)
                if n >= 2:
                    pe.wait_ge(act_vbd, n - 1)
                for j in range(4):
                    b = (s % STEPS) * SB + tl * 4 + j
                    last = pe.transpose(v_ps[q % 2][0:HK, j * EH:(j + 1) * EH], vm[:, g % 2, hf, b, :],
                                        id_s[0:EH, 0:EH])
                last.then_inc(pe_vbd, 1)

            def p_transposes(s):
                pe.wait_ge(act_exp, s + 1)
                if s >= 1:
                    pe.wait_ge(act_ct, s)
                for tl in range(2):
                    for hf in range(2):
                        last = pe.transpose(a_ps[0:HK, (tl * 2 + hf) * P:(tl * 2 + hf + 1) * P],
                                            pexp[:, tl, hf * HK:(hf + 1) * HK], id_s[:, :])
                last.then_inc(pe_pt, 1)

            def pv(s):
                pe.wait_ge(act_pt, s + 1)
                pe.wait_ge(act_vbd, 4 * s + 4)
                for tl in range(2):
                    for hf in range(2):
                        for j in range(4):
                            last = mm(a_ps[32 * j:32 * j + 32, tl * E + hf * EH:tl * E + (hf + 1) * EH],
                                      pT[:, tl, hf, 32 * j:32 * j + 32], vbd[:, tl, hf, j, :], True, True)
                last.then_inc(pe_pv, 1)

            def c_transposes(s):
                pe.wait_ge(dve_cx, s + 1)
                for tl in range(2):
                    for hf in range(2):
                        last = pe.transpose(a_ps[0:EH, (hf * 2 + tl) * P:(hf * 2 + tl + 1) * P],
                                            cx[:, tl, hf * EH:(hf + 1) * EH], id_s[:, :])
                last.then_inc(pe_ct, 1)

            def out_proj(bank, lhs, t):
                for kc in range(2):
                    last = mm(bank[:, 0:E], lhs[:, kc, t * P:(t + 1) * P], wout_s[:, kc, :], kc == 0, kc == 1)
                last.then_inc(pe_o, 1)

            def ffn1(bank, f):
                for m in range(2):
                    last = split_product(bank[:, m * GT:(m + 1) * GT], win_hi, win_lo,
                                         slice((2 * f + m) * P, (2 * f + m + 1) * P), xT2, GT)
                last.then_inc(pe_f1, 1)

            def ffn2(bank, t):
                for c in range(HC):
                    last = mm(bank[:, 0:E], gl[:, c, t * P:(t + 1) * P], w2_s[:, c, :], c == 0, c == HC - 1)
                last.then_inc(pe_f2, 1)

            for k in range(4):
                fold(k)
            pe.wait_ge(dve_cls_lo, 1)
            turn(d_ps[0], xs1, 0).then_inc(pe_cls_t, 1)
            fold(4)
            fold(5)
            pe.wait_ge(act_cls_x, 1)
            pe.wait_ge(dve_w, 1)
            for f in range(3):
                last = project(d_ps[1], f, GB, at=f * 2 * GB)
            last.then_inc(pe_cls_qkv, 1)
            fold(6)
            fold(7)
            pe.wait_ge(dve_fold, 4)

            def project_group(p, f):
                pe.wait_ge(act_x1, p + 1)
                if f < 2 and p == 0:
                    pe.wait_ge(dve_h, 2 * TILES)
                project(qkv_bank(p, f), f, GT).then_inc(pe_qkv, 1)

            def embed_group(a, t):
                if t == 0 and a >= 3:
                    pe.wait_ge(dve_h2, TILES * (a - 2))
                if a == 0:
                    pe.wait_ge(act_cls_qkv, 1)
                if a == 2 and t == 1:
                    pe.wait_ge(act_qkv, 3)
                embed(a, t, d_ps[t + (2 if a == 1 else 0)])

            def turn_group(p):
                pe.wait_ge(dve_lo, p + 1)
                if p == 0:
                    pe.wait_ge(dve_h, TILES)
                if p >= 3:
                    pe.wait_ge(dve_out, TILES * (p - 2))
                turn(turn_bank(p, 0), xs1, 0)
                turn(turn_bank(p, 1), xs1, 1).then_inc(pe_t1, 1)

            def second_ffn(e, t):
                if t == 0:
                    pe.wait_ge(act_g, 3 * e + 3)
                ffn2(d_ps[2 + t], t)

            for a in range(2):
                for t in range(TILES):
                    embed_group(a, t)
            turn_group(0)
            for f in range(3):
                project_group(0, f)

            for i in range(G):
                prj, emb, fin = i + 1 < G, i + 2 < G, i >= 1
                p, a, d = i + 1, i + 2, i - 1
                s0, s1 = STEPS * i, STEPS * i + 1
                if i == 0:
                    embed_group(a, 0)
                    embed_group(a, 1)
                scores(s0)
                if i >= 1:
                    c_transposes(s0 - 1)
                if i >= 1:
                    v_blocks(s0, 0)
                    v_blocks(s0, 1)
                if i >= 2:
                    second_ffn(i - 2, 0)
                if i == 0:
                    turn_group(p)
                if i == 0:
                    v_blocks(s0, 0)
                    v_blocks(s0, 1)
                if i >= 2:
                    second_ffn(i - 2, 1)
                if i == 0:
                    project_group(p, 0)
                if fin:
                    if d == 0:
                        pe.wait_ge(late_in, 16 * 3)
                    pe.wait_ge(act_ct, STEPS * (d + 1))
                    out_proj(d_ps[0], cT[:, d % 2], 0)
                    out_proj(d_ps[1], cT[:, d % 2], 1)
                v_blocks(s0, 2)
                v_blocks(s0, 3)
                if prj and i >= 1:
                    turn_group(p)
                p_transposes(s0)
                if i == 0:
                    project_group(p, 1)
                if emb and i >= 1:
                    embed_group(a, 0)
                pv(s0)
                if i == 0:
                    pe.wait_ge(dve_h, TILES * a + 1)
                    project_group(p, 2)
                if emb and i >= 1:
                    embed_group(a, 1)
                if prj and i >= 1:
                    project_group(p, 0)
                    project_group(p, 1)
                c_transposes(s0)
                if prj and i >= 1:
                    if emb:
                        pe.wait_ge(dve_h, TILES * a + 1)
                    else:
                        pe.wait_ge(dve_h2, TILES * d + 1)
                    project_group(p, 2)
                if fin:
                    pe.wait_ge(dve_lo2, d + 1)
                    if emb:
                        pe.wait_ge(dve_h, TILES * a + 2)
                    turn(d_ps[1], xs2, 0)
                    if prj:
                        pe.wait_ge(act_qkv, 3 * p + 1)
                    else:
                        pe.wait_ge(dve_out, TILES * d)
                    turn(d_ps[2], xs2, 1).then_inc(pe_t2, 1)
                scores(s1)
                v_blocks(s1, 0)
                v_blocks(s1, 1)
                if i == G - 1:
                    pe.wait_ge(act_ct, s0 + 1)
                    out_proj(d_ps[0], cT[:, i % 2], 0)
                if fin:
                    pe.wait_ge(act_x2, d + 1)
                    if d == 0:
                        pe.wait_ge(dve_w, 2)
                    if prj:
                        pe.wait_ge(act_qkv, 3 * p + 2)
                    ffn1(d_ps[3], 0)
                v_blocks(s1, 2)
                v_blocks(s1, 3)
                if fin:
                    if prj:
                        pe.wait_ge(act_qkv, 3 * p + 3)
                    ffn1(ffn_bank(d, 1), 1)
                p_transposes(s1)
                if i == G - 1:
                    pe.wait_ge(dve_lo2, G)
                    turn(d_ps[0], xs2, 2).then_inc(pe_t2, 1)
                if fin:
                    ffn1(d_ps[1], 2)
                pv(s1)

            def early_ffn(bank, chunks):
                for n, c in enumerate(chunks):
                    last = split_product(bank[:, n * P:(n + 1) * P], win_hi, win_lo, slice(c * P, (c + 1) * P),
                                         xT2[:, :, GT:GT + P], P)
                last.then_inc(pe_f1, 1)

            pe.wait_ge(act_x2, G)
            pe.wait_ge(act_vbd, 4 * STEPS * G)
            early_ffn(v_ps[0], range(4))
            c_transposes(STEPS * G - 1)
            early_ffn(v_ps[1], range(4, HC))
            pe.wait_ge(act_ct, STEPS * G)
            out_proj(d_ps[0], cT[:, (G - 1) % 2], 1)
            out_proj(s_ps, cTc, 0)
            second_ffn(G - 2, 0)
            second_ffn(G - 2, 1)
            pe.wait_ge(act_g, 3 * (G - 1) + 2)
            ffn2(d_ps[1], 2)
            pe.wait_ge(dve_lo2, G + 1)
            turn(d_ps[0], xs2, 0)
            turn(a_ps, xs2, 1).then_inc(pe_t2, 1)
            pe.wait_ge(act_x2, G + 1)
            pe.wait_ge(dve_out, TILES * (G - 1))
            for f in range(3):
                ffn1((d_ps[2], d_ps[3], s_ps)[f], f)
            for f in range(3):
                pe.wait_ge(act_g, 3 * (G - 1) + 2 + f + 1)
                for c in (2 * f, 2 * f + 1):
                    for t in range(2):
                        last = mm(v_ps[t][:, 0:E], gl[:, c, t * P:(t + 1) * P], w2_s[:, c, :], c == 0, c == HC - 1)
                        if c == HC - 1:
                            last.then_inc(pe_f2, 1)

        @block.scalar
        def _(act):
            act.dma_start(hcls[:], cls.partition_broadcast(P)).then_inc(cls_in, 16)
            act.dma_start(wqkv_raw[:], wqkv).then_inc(wqkv_in, 16)
            for dst, src in ((id_s[:], ident), (mask_s[:], hmask), (bqkv_s[:], bqkv),
                             (pbias_s[:], pbias.partition_broadcast(P)), (bout_s[:], bout.partition_broadcast(P))):
                act.dma_start(dst, src).then_inc(small_in, 16)

            def exp(s):
                act.wait_ge(dve_sub, s + 1)
                if s >= 1:
                    act.wait_ge(pe_pt, s)
                act.activation(pexp[:], ssub[:], ACT.Exp, scale=SCALE).then_inc(act_exp, 1)

            def p_out(s):
                act.wait_ge(pe_pt, s + 1)
                act.activation(pT[:].rearrange("p a b q -> p (a b q)"), a_ps[0:HK, :], ACT.Copy).then_inc(act_pt, 1)

            def v_out(s, q):
                n = 4 * s + q
                act.wait_ge(pe_vbd, n + 1)
                if q == 0 and s >= 1:
                    act.wait_ge(pe_pv, s)
                act.activation(vbd[:, q // 2, q % 2].rearrange("p j e -> p (j e)"),
                               v_ps[q % 2][0:HK, 0:4 * EH], ACT.Copy).then_inc(act_vbd, 1)

            def c_out(s):
                g = s // STEPS
                act.wait_ge(pe_ct, s + 1)
                if s % STEPS == 0 and g >= 2:
                    act.wait_ge(pe_o, TILES * (g - 1))
                src = a_ps[0:EH, :].rearrange("p (h b q) -> p h b q", h=2, q=32)
                dst = cT[:, g % 2, :, (s % STEPS) * P:(s % STEPS + 1) * P].rearrange("p h (b q) -> p h b q", q=NP)
                act.activation(dst, src[:, :, :, 0:NP], ACT.Copy)
                act.activation(cTc[:, :, s * SB:(s + 1) * SB], src[:, :, :, NP], ACT.Copy).then_inc(act_ct, 1)

            def with_bias(f, m, src, dst):
                return act.activation(dst, src, ACT.Identity, bias=bqkv_s[:, 2 * f + m:2 * f + m + 1])

            def images(f, r, m):
                return (qT[:, r, m, 0:QT], kT[:, m, :], vT[:, m, :])[f].rearrange("p (b t) -> p b t", t=NT)

            def qkv_out(g, f):
                act.wait_ge(pe_qkv, 3 * g + f + 1)
                if f == 0 and g >= 2:
                    act.wait_ge(pe_s, STEPS * (g - 1))
                if f > 0 and g >= 1:
                    act.wait_ge((dve_k, dve_v)[f - 1], g)
                for m in range(2):
                    src = qkv_bank(g, f)[0:EH, m * GT:(m + 1) * GT].rearrange("p (b t) -> p b t", t=NP)
                    last = with_bias(f, m, src, images(f, g % 2, m)[:, :, 0:NP])
                last.then_inc(act_qkv, 1)

            def turn_out(bank, xT, t):
                return act.activation(xT[:, :, t * P:(t + 1) * P],
                                      bank[:, 0:3 * P].rearrange("p (c t) -> p c t", c=3), ACT.Copy)

            def high(xs, xn, n, at=0):
                return act.activation(xs[:, at:at + n, 0, :], xn[:, at:at + n, :], ACT.Copy)

            def gelu(g, f):
                act.wait_ge(pe_f1, 3 * g + f + 1)
                if f == 0 and g >= 1:
                    act.wait_ge(pe_f2, TILES * g)
                for m in range(2):
                    last = act.activation(gl[:, 2 * f + m, 0:GT], ffn_bank(g, f)[:, m * GT:(m + 1) * GT],
                                          ACT.Gelu, bias=bin_s[:, 2 * f + m:2 * f + m + 1])
                last.then_inc(act_g, 1)

            act.wait_ge(small_in, 16 * 5)
            act.activation(id_r[:], id_s[:], ACT.Copy)
            act.wait_ge(dve_cls_xn, 1)
            high(xs1, xn1, 1).then_inc(act_cls_hi, 1)
            act.wait_ge(wqkv_in, 16)
            act.activation(wqkv_hi[:], wqkv_raw[:], ACT.Copy).then_inc(act_w, 1)
            act.wait_ge(pe_cls_t, 1)
            turn_out(d_ps[0], xT1, 0).then_inc(act_cls_x, 1)
            act.wait_ge(dve_init, 1)
            act.wait_ge(pe_cls_qkv, 1)
            for f in range(3):
                for m in range(2):
                    for r in range(2 if f == 0 else 1):
                        last = with_bias(f, m, d_ps[1][0:EH, (2 * f + m) * GB:(2 * f + m + 1) * GB],
                                         images(f, r, m)[:, :, NP])
            last.then_inc(act_cls_qkv, 1)

            def turned_1(p):
                act.wait_ge(pe_t1, p + 1)
                if p >= 1:
                    act.wait_ge(pe_qkv, 3 * p)
                for t in range(TILES):
                    last = turn_out(turn_bank(p, t), xT1, t)
                last.then_inc(act_x1, 1)

            def high_1(a):
                act.wait_ge(dve_xn, a + 1)
                if a >= 1:
                    act.wait_ge(pe_t1, a)
                high(xs1, xn1, TILES).then_inc(act_hi1, 1)

            high_1(0)
            turned_1(0)
            qkv_out(0, 0)
            qkv_out(0, 1)
            high_1(1)
            qkv_out(0, 2)
            for i in range(G):
                prj, emb, fin = i + 1 < G, i + 2 < G, i >= 1
                p, a, d = i + 1, i + 2, i - 1
                s0, s1 = STEPS * i, STEPS * i + 1
                if i >= 1:
                    c_out(s0 - 1)
                if i == 0:
                    turned_1(p)
                    exp(s0)
                    v_out(s0, 0)
                    v_out(s0, 1)
                else:
                    v_out(s0, 0)
                    v_out(s0, 1)
                    exp(s0)
                v_out(s0, 2)
                v_out(s0, 3)
                if prj and i >= 1:
                    turned_1(p)
                if i == 0:
                    qkv_out(p, 0)
                p_out(s0)
                if i == 0:
                    high_1(a)
                    qkv_out(p, 1)
                    qkv_out(p, 2)
                if fin:
                    act.wait_ge(dve_xn2, d + 1)
                    if d >= 1:
                        act.wait_ge(pe_t2, d)
                    high(xs2, xn2, TILES).then_inc(act_hi2, 1)
                if prj and i >= 1:
                    qkv_out(p, 0)
                    qkv_out(p, 1)
                c_out(s0)
                if emb and i >= 1:
                    high_1(a)
                if prj and i >= 1:
                    qkv_out(p, 2)
                if i == 0:
                    act.wait_ge(win_in, 16)
                    act.activation(win_hi[:], win_raw, ACT.Copy).then_inc(act_w, 1)
                if fin:
                    act.wait_ge(pe_t2, d + 1)
                    if d >= 1:
                        act.wait_ge(pe_f1, 3 * d)
                    turn_out(d_ps[1], xT2, 0)
                    turn_out(d_ps[2], xT2, 1).then_inc(act_x2, 1)
                v_out(s1, 0)
                v_out(s1, 1)
                exp(s1)
                v_out(s1, 2)
                v_out(s1, 3)
                p_out(s1)
                if i == G - 1:
                    act.wait_ge(dve_xn2, G)
                    high(xs2, xn2, 1, at=2).then_inc(act_hi2, 1)
                    act.wait_ge(pe_t2, G)
                    turn_out(d_ps[0], xT2, 2).then_inc(act_x2, 1)
                if fin:
                    if d == 0:
                        act.wait_ge(late_in, 16 * 3)
                    gelu(d, 0)
                    gelu(d, 1)
                    if i < G - 1:
                        gelu(d, 2)

            c_out(STEPS * G - 1)
            gelu(G - 2, 2)
            for bank, part in ((v_ps[0], range(4)), (v_ps[1], range(4, HC))):
                act.wait_ge(pe_f1, 3 * (G - 1) + (1 if part[0] == 0 else 2))
                for n, c in enumerate(part):
                    last = act.activation(gl[:, c, GT:GT + P], bank[:, n * P:(n + 1) * P], ACT.Gelu,
                                          bias=bin_s[:, c:c + 1])
                last.then_inc(act_g, 1)
            act.wait_ge(dve_xn2, G + 1)
            act.wait_ge(pe_t2, G - 1)
            high(xs2, xn2, 2).then_inc(act_hi2, 1)
            act.wait_ge(pe_t2, G + 1)
            act.wait_ge(pe_f1, 3 * (G - 1))
            turn_out(d_ps[0], xT2, 0)
            turn_out(a_ps, xT2, 1).then_inc(act_x2, 1)
            act.wait_ge(pe_f2, TILES * (G - 1))
            for f in range(3):
                act.wait_ge(pe_f1, 3 * (G - 1) + 2 + f + 1)
                for m in range(2):
                    last = act.activation(gl[:, 2 * f + m, 0:GT], (d_ps[2], d_ps[3], s_ps)[f][:, m * GT:(m + 1) * GT],
                                          ACT.Gelu, bias=bin_s[:, 2 * f + m:2 * f + m + 1])
                last.then_inc(act_g, 1)

        @block.vector
        def _(dve):
            linked = [0]

            def link(ins):
                linked[0] += 1
                ins.then_inc(dve_chain, 1)
                dve.wait_ge(dve_chain, linked[0])

            def stats(src, ln, n, at=0):
                for t in range(at, at + n):
                    link(dve.bn_stats(st[:, ln, t, :], src(t)))
                for t in range(at, at + n):
                    ins = dve.bn_aggr(mv[:, ln, t, :], st[:, ln, t, :])
                link(ins)
                dve.tensor_scalar(ve[:, ln, at:at + n], mv[:, ln, at:at + n, 1], EPS, None,
                                  ALU.add).then_inc(dve_ve, 1)

            def normalise(src, dst, ln, n, what, at=0):
                dve.wait_ge(pool_rstd, nth[what])
                for t in range(at, at + n):
                    ins = dve.tensor_scalar(dst[:, t, :], src(t), mv[:, ln, t, 0:1], rstd[:, ln, t:t + 1],
                                            ALU.subtract, ALU.mult)
                return ins

            def low(xs, xn, n, at=0):
                return dve.tensor_tensor(xs[:, at:at + n, 1, :], xn[:, at:at + n, :],
                                         xs[:, at:at + n, 0, :].bitcast(F32), ALU.subtract)

            def softmax_top(s):
                dve.wait_ge(pe_s, s + 1)
                sc = s_ps[:, 0:2 * HEADS * NT].rearrange("p (h k) -> p h k", k=NT)
                link(dve.tensor_reduce(smax[:], sc, AX.X, ALU.max))
                if s >= 1:
                    dve.wait_ge(act_exp, s)
                dve.tensor_tensor(ssub[:].rearrange("p a (h k) -> p (a h) k", k=NT), sc,
                                  smax[:].unsqueeze(2).to_broadcast([P, 2 * HEADS, NT]),
                                  ALU.subtract).then_inc(dve_sub, 1)

            def softmax_sum(s):
                dve.wait_ge(act_exp, s + 1)
                link(dve.tensor_reduce(ssum[:], pexp[:].rearrange("p a (h k) -> p (a h) k", k=NT), AX.X, ALU.add))
                dve.reciprocal(rinv[:], ssum[:]).then_inc(dve_chain, 1)
                linked[0] += 1
                return linked[0]

            def context(s, summed):
                dve.wait_ge(pe_pv, s + 1)
                dve.wait_ge(dve_chain, summed)
                if s >= 1:
                    dve.wait_ge(pe_ct, s)
                dve.tensor_tensor(cx[:].rearrange("p a (h d) -> p (a h) d", d=DK),
                                  a_ps[:, 0:2 * E].rearrange("p (h d) -> p h d", d=DK),
                                  rinv[:].unsqueeze(2).to_broadcast([P, 2 * HEADS, DK]),
                                  ALU.mult).then_inc(dve_cx, 1)

            def masks(g, src, dst, f, done):
                dve.wait_ge(act_qkv, 3 * g + f + 1)
                if g >= 2:
                    if f == 1:
                        dve.wait_ge(pe_s, STEPS * (g - 1))
                    else:
                        dve.wait_ge(pe_vbd, 4 * STEPS * (g - 1))
                for h in range(HH):
                    ins = dve.tensor_scalar(
                        dst[:, g % 2, :, :, h * NT:(h + 1) * NT].rearrange("p a b t -> p (a b) t"),
                        src[:].rearrange("p a (b t) -> p (a b) t", t=NT), mask_s[:, h:h + 1], None, ALU.mult)
                ins.then_inc(done, 1)

            dve.memset(mhalf[:], -0.5)
            for r in range(2):
                for m in range(2):
                    ins = dve.memset(qT[:, r, m, QT:QW], 0.0)
            ins.then_inc(dve_init, 1)
            dve.wait_ge(cls_in, 16)
            stats(lambda t: hcls[:], 0, 1)
            normalise(lambda t: hcls[:], xn1, 0, 1, ("cls", 0)).then_inc(dve_cls_xn, 1)
            dve.wait_ge(act_cls_hi, 1)
            low(xs1, xn1, 1).then_inc(dve_cls_lo, 1)
            dve.wait_ge(act_w, 1)
            dve.tensor_tensor(wqkv_lo[:], wqkv_raw[:, 0:2], wqkv_hi[:, 0:2].bitcast(F32),
                              ALU.subtract).then_inc(dve_w, 1)
            for n in range(4):
                dve.wait_ge(pe_fold, n + 1)
                dve.tensor_copy(wf[:, n // 2].rearrange("p c e -> p (c e)")[:, (n % 2) * 288:(n % 2 + 1) * 288],
                                fold_ps[n][:, 0:288]).then_inc(dve_fold, 1)
            dve.wait_ge(small_in, 16 * 5)

            def embedded(a, t):
                dve.wait_ge(pe_embed, TILES * a + t + 1)
                if a >= 1 and t == 0:
                    dve.wait_ge(pool_hb, a)
                dve.tensor_tensor(h_s[:, t, :], d_ps[t + (2 if a == 1 else 0)][:, 0:E], pbias_s[:],
                                  ALU.add).then_inc(dve_h, 1)

            def norm_stats_1(a):
                dve.wait_ge(dve_h, TILES * (a + 1))
                stats(lambda t: h_s[:, t, :], 0, TILES)

            def norm_1(a):
                if a >= 1:
                    dve.wait_ge(act_hi1, a)
                normalise(lambda t: h_s[:, t, :], xn1, 0, TILES, ("ln1", a)).then_inc(dve_xn, 1)

            def low_1(a):
                dve.wait_ge(dve_xn, a + 1)
                dve.wait_ge(act_hi1, a + 1)
                low(xs1, xn1, TILES).then_inc(dve_lo, 1)

            def finished(e, t):
                if e >= 2 and t == 0:
                    dve.wait_ge(out_done[e % 2], 16 * (e // 2))
                dve.wait_ge(pe_f2, TILES * e + t + 1)
                dve.tensor_tensor(os_[:, e % 2, t, :], d_ps[2 + t][:, 0:E], h2[:, e % 2, t, :],
                                  ALU.add).then_inc(dve_out, 1)

            for t in range(TILES):
                embedded(0, t)
            norm_stats_1(0)
            norm_1(0)
            low_1(0)
            for t in range(TILES):
                embedded(1, t)
            norm_stats_1(1)
            norm_1(1)
            dve.wait_ge(act_cls_qkv, 1)
            masks(0, kT, kbd, 1, dve_k)
            low_1(1)
            masks(0, vT, vm, 2, dve_v)
            for i in range(G):
                prj, emb, fin = i + 1 < G, i + 2 < G, i >= 1
                p, a, d = i + 1, i + 2, i - 1
                s0, s1 = STEPS * i, STEPS * i + 1
                softmax_top(s0)
                if i == 0:
                    embedded(a, 0)
                    embedded(a, 1)
                if i >= 2:
                    finished(i - 2, 0)
                summed = softmax_sum(s0)
                if i >= 2:
                    finished(i - 2, 1)
                if i == 0:
                    norm_stats_1(a)
                    norm_1(a)
                if fin:
                    dve.wait_ge(pool_hb, d + 1)
                    for t in range(TILES):
                        dve.wait_ge(pe_o, TILES * d + t + 1)
                        dve.tensor_tensor(h2[:, d % 2, t, :], d_ps[t][:, 0:E], hb_s[:, d, t, :],
                                          ALU.add).then_inc(dve_h2, 1)
                    dve.wait_ge(dve_h2, TILES * (d + 1))
                    stats(lambda t: h2[:, d % 2, t, :], 1, TILES)
                    if d >= 1:
                        dve.wait_ge(act_hi2, d)
                    normalise(lambda t: h2[:, d % 2, t, :], xn2, 1, TILES, ("ln2", d)).then_inc(dve_xn2, 1)
                    dve.wait_ge(dve_xn2, d + 1)
                if emb and i >= 1:
                    embedded(a, 0)
                context(s0, summed)
                if fin:
                    dve.wait_ge(act_hi2, d + 1)
                    low(xs2, xn2, TILES).then_inc(dve_lo2, 1)
                if emb and i >= 1:
                    embedded(a, 1)
                    norm_stats_1(a)
                    norm_1(a)
                if prj:
                    masks(p, kT, kbd, 1, dve_k)
                if emb:
                    low_1(a)
                softmax_top(s1)
                if i == 0:
                    dve.wait_ge(act_w, 2)
                    dve.tensor_tensor(win_lo[:], win_raw[:, 0:2], win_hi[:, 0:2].bitcast(F32),
                                      ALU.subtract).then_inc(dve_w, 1)
                if i == G - 1:
                    dve.wait_ge(pe_o, TILES * i + 1)
                    dve.wait_ge(pool_hb, i + 1)
                    link(dve.tensor_tensor(h2[:, i % 2, 0, :], d_ps[0][:, 0:E], hb_s[:, i, 0, :], ALU.add))
                    stats(lambda t: h2[:, i % 2, 0, :], 1, 1, at=2)
                summed = softmax_sum(s1)
                if i == G - 1:
                    normalise(lambda t: h2[:, i % 2, 0, :], xn2, 1, 1, ("early", 0), at=2).then_inc(dve_xn2, 1)
                    dve.wait_ge(dve_xn2, G)
                    dve.wait_ge(act_hi2, G)
                    low(xs2, xn2, 1, at=2).then_inc(dve_lo2, 1)
                if prj:
                    masks(p, vT, vm, 2, dve_v)
                context(s1, summed)

            d = G - 1
            last_h2 = [h2[:, d % 2, 1, :], h2c[:]]
            for t in range(2):
                dve.wait_ge(pe_o, TILES * d + t + 2)
                ins = dve.tensor_tensor(last_h2[t], (d_ps[0], s_ps)[t][:, 0:E], (hb_s[:, d, 1, :], hbcls[:])[t],
                                        ALU.add)
            link(ins)
            stats(lambda t: last_h2[t], 1, 2)
            dve.wait_ge(act_hi2, G - 1)
            normalise(lambda t: last_h2[t], xn2, 1, 2, ("ln2", d)).then_inc(dve_xn2, 1)
            finished(G - 2, 0)
            dve.wait_ge(dve_xn2, G + 1)
            dve.wait_ge(act_hi2, G + 1)
            low(xs2, xn2, 2).then_inc(dve_lo2, 1)
            finished(G - 2, 1)
            dve.wait_ge(out_done[d % 2], 16 * (d // 2))
            dve.wait_ge(pe_f2, TILES * d + 1)
            dve.tensor_tensor(os_[:, d % 2, 0, :], d_ps[1][:, 0:E], h2[:, d % 2, 0, :], ALU.add).then_inc(dve_out, 1)
            for t in range(2):
                dve.wait_ge(pe_f2, TILES * d + t + 2)
                dve.tensor_tensor((os_[:, d % 2, 1, :], osc[:])[t], v_ps[t][:, 0:E], last_h2[t],
                                  ALU.add).then_inc(dve_out, 1)

        @block.gpsimd
        def _(pool):
            def inverse_root(ln, n, what, at=0):
                pool.wait_ge(dve_ve, nth[what])
                pool.tensor_tensor(rstd[:, ln, at:at + n], ve[:, ln, at:at + n], mhalf[:, 0:n],
                                   ALU.pow).then_inc(pool_rstd, 1)

            pool.wait_ge(dve_init, 1)
            inverse_root(0, 1, ("cls", 0))
            pool.wait_ge(small_in, 16 * 5)
            pool.wait_ge(cls_in, 16)
            pool.tensor_tensor(hbcls[:], hcls[:], bout_s[:], ALU.add)
            for i in ITER:
                a, d = i + 2, i - 1
                if d >= 0:
                    inverse_root(1, TILES, ("ln2", d))
                if i == G - 1:
                    inverse_root(1, 1, ("early", 0), at=2)
                if a < G:
                    inverse_root(0, TILES, ("ln1", a))
                    pool.tensor_tensor(hb_s[:, a], h_s[:], bout_s[:].unsqueeze(1).to_broadcast([P, TILES, E]),
                                       ALU.add).then_inc(pool_hb, 1)


def kernel(x, cls_tok, L0_tok_proj_weight, L0_tok_proj_bias, L0_tok_pinv, L0_attn_w_qkv, L0_attn_b_qkv,
           L0_attn_w_out, L0_attn_b_out, L0_ffn_in_weight, L0_ffn_in_bias, L0_ffn_out_weight):
    import numpy as np
    import concourse.bacc as bacc
    from concourse.bass_utils import run_bass_kernel_spmd

    def lay(a):
        return np.ascontiguousarray(a)

    def chunks(w):
        return np.concatenate([w, w], axis=0).reshape(3, P, -1).transpose(1, 0, 2)

    xp = np.asarray(x).reshape(G, GB, C, 4, 16, 4, 16).transpose(0, 2, 4, 6, 1, 3, 5)
    xp = xp.reshape(G, XC, P, GT).transpose(0, 2, 1, 3)
    wt = np.asarray(L0_tok_proj_weight).reshape(E, C, OC, P).transpose(3, 2, 1, 0).reshape(P, OC, C * E)
    pinvt = np.asarray(L0_tok_pinv).reshape(PIX, OC, P).transpose(2, 1, 0)
    arrays = {
        "xt": lay(xp), "wt": lay(wt), "pinvt": lay(pinvt),
        "pbias": lay(L0_tok_proj_bias), "cls": lay(np.asarray(cls_tok).reshape(E)),
        "wqkv": lay(chunks(np.asarray(L0_attn_w_qkv))),
        "bqkv": lay(np.asarray(L0_attn_b_qkv).reshape(6, EH).T),
        "wout": lay(np.asarray(L0_attn_w_out).reshape(2, EH, E).transpose(1, 0, 2)),
        "bout": lay(L0_attn_b_out),
        "win": lay(chunks(np.asarray(L0_ffn_in_weight).T)),
        "bin_": lay(np.asarray(L0_ffn_in_bias).reshape(HC, P).T),
        "w2": lay(np.asarray(L0_ffn_out_weight).reshape(HC, P, E).transpose(1, 0, 2)),
        "ident": np.eye(P, dtype=np.float32),
        "hmask": np.repeat(np.eye(HH, dtype=np.float32), DK, axis=0),
    }
    nc = bacc.Bacc("TRN2", target_bir_lowering=False, num_devices=1)
    args = [nc.dram_tensor(n, a.shape, F32, kind="ExternalInput").ap() for n, a in arrays.items()]
    out_p = nc.dram_tensor("out_p", [G, P, TILES, E], F32, kind="ExternalOutput").ap()
    out_c = nc.dram_tensor("out_c", [B, E], F32, kind="ExternalOutput").ap()
    vit_tower(nc, *args, out_p, out_c)
    r = run_bass_kernel_spmd(nc, [arrays], core_ids=[0]).results[0]
    patches = np.asarray(r["out_p"]).transpose(0, 2, 1, 3).reshape(B, NP, E)
    return np.concatenate([np.asarray(r["out_c"]).reshape(B, 1, E), patches], axis=1)
```

```python
from contextlib import ExitStack

import concourse.bass as bass
from concourse import mybir

F32 = mybir.dt.float32
F32R = mybir.dt.float32r
ALU = mybir.AluOpType
ACT = mybir.ActivationFunctionType
AX = mybir.AxisListType

P = 128
E = 192
EH = E // 2
HEADS, DK = 12, 16
HH = HEADS // 2
B, C, PIX = 128, 3, 256
OLD = 1024
NP, NT = 16, 17
GB = 16
G = B // GB
GT = GB * NP
TILES = GT // P
CW = 2 * GB
QT = GB * NT
QW = QT + 32 - NT
SB = 8
STEPS = GB // SB
HK = HH * NT
HID = 768
HC = HID // P
XSLOTS = 3
XC = C * PIX // P
OC = OLD // P
EPS = 1e-5
SCALE = DK ** -0.5
WARM = 2


def vit_tower(nc, xt, wt, pinvt, pbias, cls, wqkv, bqkv, bv, wout, bout, win, bin_, w2, ident, hmask, v_dram, vcls_dram,
              out_p, out_c):
    with ExitStack() as ctx:
        def sb(name, shape, dt=F32):
            return ctx.enter_context(nc.sbuf_tensor(name, shape, dt))

        def pb(name):
            return ctx.enter_context(nc.psum_tensor(name, [P, 512], F32))

        def sem(name):
            return ctx.enter_context(nc.semaphore(name))

        wt_s = sb("wt_s", [P, OC, C * E])
        pinv_s = sb("pinv_s", [P, OC, PIX])
        wf = sb("wf", [P, 2, C, E])
        wqkv_raw = sb("wqkv_raw", [P, 3, 3 * E])
        wqkv_hi = sb("wqkv_hi", [P, 3, 3 * E], F32R)
        wqkv_lo = sb("wqkv_lo", [P, 2, 3 * E], F32R)
        win_hi = sb("win_hi", [P, 3, HID], F32R)
        win_lo = sb("win_lo", [P, 2, HID], F32R)
        bqkv_s = sb("bqkv_s", [EH, 6])
        wout_s = sb("wout_s", [EH, 2, E])
        bin_s = sb("bin_s", [P, HC])
        w2_s = sb("w2_s", [P, HC, 2, E], F32R)
        pbias_s = sb("pbias_s", [P, E])
        bout_s = sb("bout_s", [P, E])
        bv_s = sb("bv_s", [P, E])
        id_s = sb("id_s", [P, P])
        id_r = sb("id_r", [P, P], F32R)
        mask_s = sb("mask_s", [EH, HH])
        mhalf = sb("mhalf", [P, TILES + 1])
        x_s = sb("x_s", [P, XSLOTS, XC, GT])
        h_s = sb("h_s", [P, 2, TILES, E])
        hcls = sb("hcls", [P, E])
        hb_s = sb("hb_s", [P, 4, TILES, E])
        hbcls = sb("hbcls", [P, E])
        st = sb("st", [P, 2, TILES + 1, 6])
        mv = sb("mv", [P, 2, TILES + 1, 2])
        ve = sb("ve", [P, 2, TILES + 1])
        rstd = sb("rstd", [P, 2, TILES + 1])
        xn1 = sb("xn1", [P, TILES, E])
        xn2 = sb("xn2", [P, TILES + 1, E])
        xs1 = sb("xs1", [P, TILES, 2, E], F32R)
        xs2 = sb("xs2", [P, TILES + 1, 2, E], F32R)
        xT1 = sb("xT1", [P, 3, GT + CW], F32R)
        xT2 = sb("xT2", [P, 3, GT + P], F32R)
        qT = sb("qT", [EH, 2, 2, QW])
        kT = sb("kT", [EH, 2, QT])
        vcls = sb("vcls", [CW, E])
        kbd = sb("kbd", [EH, 2, GB, HK])
        vbd = sb("vbd", [HK, 2, GB, 2, EH])
        ssub = sb("ssub", [P, 2, HEADS * NT])
        pexp = sb("pexp", [P, 2, HEADS * NT])
        smax = sb("smax", [P, 2 * HEADS])
        ssum = sb("ssum", [P, 2 * HEADS])
        rinv = sb("rinv", [P, 2 * HEADS])
        pT = sb("pT", [HK, 2, 2, 2, P])
        cT = sb("cT", [EH, 2, 2, GT])
        cTc = sb("cTc", [EH, 2, B])
        h2 = sb("h2", [P, 2, TILES, E])
        h2c = sb("h2c", [P, E])
        win_raw = wt_s[:, 0:4, :].rearrange("p a b -> p (a b)").rearrange("p (c h) -> p c h", c=3)
        spare = wt_s[:, 4:8, :].rearrange("p a b -> p (a b)")
        v_tok = spare[:, 0:2 * E].rearrange("p (t e) -> p t e", t=TILES)
        cx = spare[:, 2 * E:4 * E].rearrange("p (t e) -> p t e", t=2)
        os_ = spare[:, 4 * E:8 * E].rearrange("p (r t e) -> p r t e", r=2, t=TILES)
        gl_raw = pinv_s[:].rearrange("p a b -> p (a b)").rearrange("p (r n) -> p r n", n=512)
        w2_raw = wqkv_raw[:].rearrange("p a b -> p (a b)")[:, 0:HC * E].rearrange("p (c e) -> p c e", c=HC)
        gl = [sb("gl_hi", [P, HC, GT + P], F32R), sb("gl_lo", [P, HC, GT + P], F32R)]
        osc = sb("osc", [P, E])

        d_ps = [pb("d0"), pb("d1"), pb("d2"), pb("d3")]
        s_ps, a_ps = pb("s_ps"), pb("a_ps")
        v_ps = [pb("v0"), pb("v1")]
        rest_ps = [a_ps, d_ps[2], d_ps[3]]
        fold_ps = [s_ps, a_ps, v_ps[0], v_ps[1]]

        def qkv_bank(p, f):
            if f == 2:
                return v_ps[0] if v_early(p) else d_ps[0 if p else 1]
            return d_ps[2 + f]

        def v_early(p):
            return 3 <= p < G - 1

        def half_bank(p, f, m):
            bank = (s_ps, a_ps)[f] if p == 0 and m == 1 else qkv_bank(p, f)
            return bank[:, 0:GT + CW] if p == 0 else bank[:, m * GT:(m + 1) * GT]

        def attn_bank(s):
            return v_ps[0] if s == 1 else a_ps

        def turn_bank(p, t):
            return v_ps[t] if p >= 3 else d_ps[t + (2 if p == 2 else 0)]

        def embed_bank(a, t):
            return v_ps[t] if a == 2 else d_ps[t + (2 if a == 1 else 0)]

        def ffn_bank(g, f):
            return d_ps[(3, 2 if g == G - 2 else 0, 1)[f]]

        w_in = [sem(f"w_in{k}") for k in range(OC)]
        x_in = [sem(f"x_in{r}") for r in range(XSLOTS)]
        cls_in, small_in, wqkv_in, late_in, win_in = map(sem, ("cls_in", "small_in", "wqkv_in", "late_in", "win_in"))
        v_in = [sem("v_in0"), sem("v_in1")]
        v_stored, vcls_stored, vcls_in = map(sem, ("v_stored", "vcls_stored", "vcls_in"))
        out_done = [sem("out_done0"), sem("out_done1"), sem("out_done2")]
        pe_fold, pe_embed, pe_t1, pe_qk, pe_v, pe_s, pe_pt, pe_pv, pe_ct, pe_o, pe_t2, pe_f1, pe_f2 = map(sem, (
            "pe_fold", "pe_embed", "pe_t1", "pe_qk", "pe_v", "pe_s", "pe_pt", "pe_pv", "pe_ct", "pe_o", "pe_t2",
            "pe_f1", "pe_f2"))
        pe_cls_t = sem("pe_cls_t")
        act_x1, act_qk, act_exp, act_pt, act_ct, act_x2, act_g, act_hi1, act_hi2, act_w, act_gh = map(sem, (
            "act_x1", "act_qk", "act_exp", "act_pt", "act_ct", "act_x2", "act_g", "act_hi1", "act_hi2", "act_w", "act_gh"))
        act_cls_x, act_cls_hi = map(sem, ("act_cls_x", "act_cls_hi"))
        dve_fold, dve_h, dve_xn, dve_lo, dve_k, dve_val, dve_sub, dve_cx, dve_h2, dve_xn2, dve_lo2, dve_out = map(sem, (
            "dve_fold", "dve_h", "dve_xn", "dve_lo", "dve_k", "dve_val", "dve_sub", "dve_cx", "dve_h2", "dve_xn2",
            "dve_lo2", "dve_out"))
        dve_ve, dve_chain, dve_cls_xn, dve_cls_lo, dve_cls_val, dve_init, dve_w, dve_gl = map(sem, (
            "dve_ve", "dve_chain", "dve_cls_xn", "dve_cls_lo", "dve_cls_val", "dve_init", "dve_w", "dve_gl"))
        pool_rstd, pool_hb, pool_zero, pool_w = map(sem, ("pool_rstd", "pool_hb", "pool_zero", "pool_w"))

        ITER = range(-2, G + 1)

        order = [("cls", 0)]
        for i in ITER:
            if i >= 1:
                order.append(("ln2", i - 1))
            if i == G - 1:
                order.append(("early", 0))
            if i + 2 < G:
                order.append(("ln1", i + 2))
        nth = {what: n + 1 for n, what in enumerate(order)}

        block = ctx.enter_context(nc.Block())

        @block.sync
        def _(sp):
            def load_x(g):
                if g >= XSLOTS:
                    sp.wait_ge(pe_embed, TILES * (g - XSLOTS + 1))
                sp.dma_start(x_s[:, g % XSLOTS], xt[g]).then_inc(x_in[g % XSLOTS], 16)

            for k in range(OC):
                sp.dma_start(wt_s[:, k], wt[:, k]).then_inc(w_in[k], 16)
                if k % 2 == 0:
                    sp.dma_start(pinv_s[:, k:k + 2], pinvt[:, k:k + 2]).then_inc(w_in[k], 16)
            load_x(0)
            load_x(1)
            load_x(2)

            sp.wait_ge(dve_cls_val, 1)
            sp.dma_start(vcls_dram, vcls[:]).then_inc(vcls_stored, 16)
            sp.wait_ge(pool_zero, 1)
            sp.wait_ge(vcls_stored, 16)
            for h in range(HH):
                sp.dma_start(vbd[h * NT + NP:h * NT + NT, :, :, :, h * DK:(h + 1) * DK].rearrange(
                    "p r b f d -> p (r b f) d"), vcls_dram.rearrange(
                        "i (f d) -> (i f) d", f=2)[:, h * DK:(h + 1) * DK].unsqueeze(0)).then_inc(vcls_in, 16)

            def place_v(g):
                sp.wait_ge(dve_val, g + 1)
                sp.dma_start(v_dram[g].rearrange("(t p) e -> p t e", p=P), v_tok).then_inc(v_stored, 16)
                if g >= 2:
                    sp.wait_ge(pe_pv, STEPS * (g - 1))
                sp.wait_ge(v_stored, 16 * (g + 1))
                for h in range(HH):
                    for hf in range(2):
                        at = hf * EH + h * DK
                        sp.dma_start(vbd[h * NT:h * NT + NP, g % 2, :, hf, h * DK:(h + 1) * DK],
                                     v_dram[g].rearrange("(b t) e -> t b e", t=NP)[:, :, at:at + DK]
                                     ).then_inc(v_in[g % 2], 16)

            sp.wait_ge(pe_fold, 4)
            sp.dma_start(win_raw, win).then_inc(win_in, 16)
            sp.wait_ge(act_w, 1)
            sp.wait_ge(dve_w, 1)
            for dst, src in ((wout_s[:], wout), (bin_s[:], bin_), (w2_raw, w2)):
                sp.dma_start(dst, src).then_inc(late_in, 16)
            load_x(3)
            load_x(4)
            place_v(0)
            for i in range(G + 2):
                if i >= 2:
                    sp.wait_ge(dve_out, TILES * (i - 1))
                    sp.dma_start(out_p[i - 2], os_[:, i % 2]).then_inc(out_done[i % 2], 16)
                if i + 5 < G:
                    load_x(i + 5)
                if i + 1 < G:
                    place_v(i + 1)
            sp.wait_ge(dve_out, TILES * G + 1)
            sp.dma_start(out_c, osc[:]).then_inc(out_done[2], 16)
            sp.wait_ge(out_done[0], 16 * (G // 2))
            sp.wait_ge(out_done[1], 16 * (G // 2))
            sp.wait_ge(out_done[2], 16)

        @block.tensor
        def _(pe):
            def mm(out, lhsT, rhs, start, stop):
                return pe.matmul(out, lhsT, rhs, start=start, stop=stop)

            def split_product(out, hi, lo, cols, xT, n):
                mm(out, hi[:, 0, cols], xT[:, 0, 0:n], True, False)
                mm(out, lo[:, 0, cols], xT[:, 0, 0:n], False, False)
                mm(out, lo[0:E - P, 1, cols], xT[0:E - P, 1, 0:n], False, False)
                mm(out, hi[:, 1, cols], xT[:, 1, 0:n], False, False)
                return mm(out, hi[:, 2, cols], xT[:, 2, 0:n], False, True)

            def fold(k):
                pe.wait_ge(w_in[k], 32 if k % 2 == 0 else 16)
                for ph in range(2):
                    for n in range(2):
                        last = mm(fold_ps[2 * ph + n][:, 0:288], pinv_s[:, k, ph * P:(ph + 1) * P],
                                  wt_s[:, k, n * 288:(n + 1) * 288], k == 0, k == OC - 1)
                        if k == OC - 1:
                            last.then_inc(pe_fold, 1)

            def embed(g, t, bank):
                if t == 0:
                    pe.wait_ge(x_in[g % XSLOTS], 16 * (g // XSLOTS + 1))
                for c in range(XC):
                    last = mm(bank[:, 0:E], x_s[:, g % XSLOTS, c, t * P:(t + 1) * P], wf[:, c % 2, c // 2, :],
                              c == 0, c == XC - 1)
                last.then_inc(pe_embed, 1)

            def turn(bank, xs, t):
                src = xs[:, t].rearrange("p a e -> p (a e)")
                for c in range(3):
                    last = pe.transpose(bank[:, c * P:(c + 1) * P].bitcast(F32R), src[:, c * P:(c + 1) * P], id_r[:, :])
                return last

            def project_v(bank, t, at):
                cols, tok = slice(2 * E, 3 * E), slice(t * P, (t + 1) * P if t < TILES else GT + CW)
                out = bank[0:tok.stop - tok.start, at:at + E]
                x0, x1, x2 = (xT1[:, c, tok] for c in range(3))
                mm(out, x0, wqkv_hi[:, 0, cols], True, False)
                mm(out, x0, wqkv_lo[:, 0, cols], False, False)
                mm(out, xT1[0:E - P, 1, tok], wqkv_lo[0:E - P, 1, cols], False, False)
                mm(out, x1, wqkv_hi[:, 1, cols], False, False)
                return mm(out, x2, wqkv_hi[:, 2, cols], False, True)

            def project(g, f):
                n = GT + (CW if g == 0 else 0)
                for m in range(2):
                    last = split_product(half_bank(g, f, m)[0:EH, :], wqkv_hi, wqkv_lo,
                                         slice(f * E + m * EH, f * E + (m + 1) * EH), xT1, n)
                return last

            def scores(s):
                g = s // STEPS
                pe.wait_ge(dve_k, g + 1)
                pe.wait_ge(act_qk, 2 * g + 2)
                if s >= 1:
                    pe.wait_ge(dve_sub, s)
                for tl in range(2):
                    for j in range(4):
                        b = (s % STEPS) * SB + tl * 4 + j
                        for hf in range(2):
                            last = mm(s_ps[32 * j:32 * j + 32, tl * 204 + hf * HK:tl * 204 + (hf + 1) * HK],
                                      qT[:, g % 2, hf, b * NT:b * NT + 32], kbd[:, hf, b, :], True, True)
                last.then_inc(pe_s, 1)

            def p_transposes(s):
                pe.wait_ge(act_exp, s + 1)
                if s >= 2:
                    pe.wait_ge(act_ct, s)
                for tl in range(2):
                    for hf in range(2):
                        last = pe.transpose(attn_bank(s)[0:HK, (tl * 2 + hf) * P:(tl * 2 + hf + 1) * P],
                                            pexp[:, tl, hf * HK:(hf + 1) * HK], id_s[:, :])
                last.then_inc(pe_pt, 1)

            def pv(s):
                g = s // STEPS
                pe.wait_ge(act_pt, s + 1)
                if s % STEPS == 0:
                    pe.wait_ge(v_in[g % 2], 16 * 2 * HH * (g // 2 + 1))
                if s == 0:
                    pe.wait_ge(vcls_in, 16 * HH)
                for tl in range(2):
                    for hf in range(2):
                        for j in range(4):
                            last = mm(attn_bank(s)[32 * j:32 * j + 32, tl * E + hf * EH:tl * E + (hf + 1) * EH],
                                      pT[:, s % 2, tl, hf, 32 * j:32 * j + 32],
                                      vbd[:, g % 2, (s % STEPS) * SB + tl * 4 + j, hf, :], True, True)
                last.then_inc(pe_pv, 1)

            def c_transposes(s):
                pe.wait_ge(dve_cx, s + 1)
                for tl in range(2):
                    for hf in range(2):
                        last = pe.transpose(attn_bank(s)[0:EH, (hf * 2 + tl) * P:(hf * 2 + tl + 1) * P],
                                            cx[:, tl, hf * EH:(hf + 1) * EH], id_s[:, :])
                last.then_inc(pe_ct, 1)

            def out_proj(bank, lhs, t):
                for kc in range(2):
                    last = mm(bank[:, 0:E], lhs[:, kc, t * P:(t + 1) * P], wout_s[:, kc, :], kc == 0, kc == 1)
                last.then_inc(pe_o, 1)

            def ffn1(bank, f):
                for m in range(2):
                    last = split_product(bank[:, m * GT:(m + 1) * GT], win_hi, win_lo,
                                         slice((2 * f + m) * P, (2 * f + m + 1) * P), xT2, GT)
                last.then_inc(pe_f1, 1)

            def high_product(bank, c, t):
                return mm(bank[:, 0:2 * E], gl[0][:, c, t * P:(t + 1) * P], w2_s[:, c].rearrange("p r e -> p (r e)"),
                          c == 0, c == HC - 1)

            def low_product(bank, c, t):
                return mm(bank[:, 0:E], gl[1][:, c, t * P:(t + 1) * P], w2_s[:, c, 0], False, False)

            def ffn2(bank, t, parts):
                for split, chunks in parts:
                    pe.wait_ge(act_gh, split)
                    for c in chunks:
                        if c < HC - 1:
                            high_product(bank, c, t)
                for split, chunks in parts:
                    pe.wait_ge(dve_gl, split)
                    for c in chunks:
                        low_product(bank, c, t)
                high_product(bank, HC - 1, t).then_inc(pe_f2, 1)

            pe.wait_ge(dve_init, 1)
            for n in range(WARM):
                mm(d_ps[3][0:EH, :], cT[:, 0, 0, 0:EH], cT[:, 0].rearrange("p h t -> p (h t)"), True, True)

            for k in range(4):
                fold(k)
            pe.wait_ge(dve_cls_lo, 1)
            turn(d_ps[0], xs1, 0).then_inc(pe_cls_t, 1)
            fold(4)
            fold(5)
            pe.wait_ge(act_cls_x, 1)
            pe.wait_ge(dve_w, 1)
            project_v(d_ps[2], TILES, 0).then_inc(pe_v, 1)
            fold(6)
            fold(7)
            pe.wait_ge(dve_fold, 4)

            def project_group(p, f):
                pe.wait_ge(act_x1, p + 1)
                if f < 2 and p == 0:
                    pe.wait_ge(dve_h, 2 * TILES)
                if f < 2 and p == 1:
                    pe.wait_ge(act_qk, 2 - f)
                if f < 2 and p >= 3:
                    pe.wait_ge(dve_out, TILES * (p - 2))
                if f == 2 and p >= 2 and not v_early(p):
                    pe.wait_ge(dve_h2, TILES * (p - 1))
                if f < 2:
                    project(p, f).then_inc(pe_qk, 1)
                else:
                    for t in range(TILES):
                        last = project_v(qkv_bank(p, f), t, t * E)
                    last.then_inc(pe_v, 1)

            def embed_group(a, t):
                if a == 3:
                    pe.wait_ge(dve_val, 2)
                elif a >= 3:
                    pe.wait_ge(dve_h2, TILES * (a - 3) + t + 1)
                if a == 0:
                    pe.wait_ge(dve_cls_val, 1)
                embed(a, t, embed_bank(a, t))

            def turn_group(p):
                pe.wait_ge(dve_lo, p + 1)
                if p == 0:
                    pe.wait_ge(dve_h, TILES)
                if p == 1:
                    pe.wait_ge(dve_val, 1)
                if p == 2:
                    pe.wait_ge(act_qk, 2 * p)
                if p >= 3:
                    pe.wait_ge(act_x2, p - 2)
                turn(turn_bank(p, 0), xs1, 0)
                turn(turn_bank(p, 1), xs1, 1).then_inc(pe_t1, 1)

            def second_ffn(e, t):
                if e == 0 and t == 0:
                    pe.wait_ge(pool_w, 2)
                ffn2(d_ps[2 + t], t, [(3 * e + f + 1, (2 * f, 2 * f + 1)) for f in range(3)])

            for a in range(2):
                for t in range(TILES):
                    embed_group(a, t)
            embed_group(2, 0)
            turn_group(0)
            embed_group(2, 1)
            for f in (1, 2, 0):
                project_group(0, f)

            for i in range(G):
                prj, emb = i + 1 < G, i + 2 < G
                p, a, d = i + 1, i + 2, i - 1
                s0, s1 = STEPS * i, STEPS * i + 1
                if i == 0:
                    turn_group(p)
                    project_group(p, 1)
                if i == 1:
                    embed_group(a, 1)
                scores(s0)
                if i == 0:
                    project_group(p, 2)
                    project_group(p, 0)
                    p_transposes(s0)
                    scores(s1)
                    embed_group(a + 1, 0)
                    pv(s0)
                    p_transposes(s1)
                    c_transposes(s0)
                    pv(s1)
                    continue
                if i == 1:
                    c_transposes(s0 - 1)
                if prj:
                    turn_group(p)
                if i >= 2:
                    second_ffn(i - 2, 0)
                if 2 <= i < G - 1:
                    second_ffn(i - 2, 1)
                if d == 0:
                    pe.wait_ge(late_in, 16 * 3)
                pe.wait_ge(act_ct, STEPS * (d + 1))
                pe.wait_ge(act_g, 3 * d)
                if i == 1:
                    pe.wait_ge(dve_h, TILES * a + 1)
                out_proj(d_ps[0], cT[:, d % 2], 0)
                if i == 1:
                    pe.wait_ge(dve_h, TILES * a + 2)
                out_proj(d_ps[1], cT[:, d % 2], 1)
                p_transposes(s0)
                if v_early(p):
                    project_group(p, 2)
                if emb and i >= 2:
                    embed_group(a, 0)
                elif prj:
                    project_group(p, 1)
                pv(s0)
                scores(s1)
                if emb and i >= 2:
                    embed_group(a, 1)
                elif i == G - 2:
                    project_group(p, 2)
                elif i == G - 1:
                    second_ffn(i - 2, 1)
                if emb and i >= 2:
                    pe.wait_ge(dve_lo2, d + 1)
                    turn(v_ps[0], xs2, 0)
                    turn(v_ps[1], xs2, 1).then_inc(pe_t2, 1)
                c_transposes(s0)
                if not emb:
                    pe.wait_ge(dve_lo2, d + 1)
                    turn(v_ps[0], xs2, 0)
                    turn(v_ps[1], xs2, 1).then_inc(pe_t2, 1)
                if emb and i >= 2:
                    project_group(p, 1)
                if i == 1:
                    pe.wait_ge(dve_h, TILES * a + 1)
                    project_group(p, 2)
                    pe.wait_ge(dve_lo2, d + 1)
                    turn(v_ps[0], xs2, 0)
                    turn(v_ps[1], xs2, 1).then_inc(pe_t2, 1)
                if i == G - 2:
                    project_group(p, 0)
                p_transposes(s1)
                if emb:
                    project_group(p, 0)
                if i == G - 1:
                    pe.wait_ge(act_ct, s0 + 1)
                    out_proj(d_ps[0], cT[:, i % 2], 0)
                if i != G - 2:
                    pv(s1)
                pe.wait_ge(act_x2, d + 1)
                if d == 0:
                    pe.wait_ge(pool_w, 1)
                if prj:
                    pe.wait_ge(act_qk, 2 * p + 1)
                else:
                    pe.wait_ge(dve_out, TILES * d)
                ffn1(d_ps[3], 0)
                if i == G - 2:
                    pv(s1)
                if v_early(p):
                    pe.wait_ge(dve_h, TILES * a + 1)
                elif prj:
                    pe.wait_ge(dve_val, p + 1)
                if i == G - 1:
                    c_transposes(s1)
                ffn1(ffn_bank(d, 1), 1)
                if emb:
                    pe.wait_ge(dve_h, TILES * a + 2)
                ffn1(ffn_bank(d, 2), 2)
                if i < G - 1:
                    c_transposes(s1)
                if i == G - 1:
                    pe.wait_ge(dve_lo2, G)
                    turn(d_ps[0], xs2, 2).then_inc(pe_t2, 1)

            def early_ffn(bank, chunks):
                for n, c in enumerate(chunks):
                    last = split_product(bank[:, n * P:(n + 1) * P], win_hi, win_lo, slice(c * P, (c + 1) * P),
                                         xT2[:, :, GT:GT + P], P)
                last.then_inc(pe_f1, 1)

            pe.wait_ge(act_ct, STEPS * G)
            out_proj(s_ps, cT[:, (G - 1) % 2], 1)
            out_proj(a_ps, cTc, 0)
            pe.wait_ge(act_x2, G)
            early_ffn(v_ps[0], range(4))
            early_ffn(v_ps[1], range(4, HC))
            second_ffn(G - 2, 0)
            pe.wait_ge(dve_lo2, G + 1)
            turn(d_ps[0], xs2, 0)
            turn(s_ps, xs2, 1).then_inc(pe_t2, 1)
            second_ffn(G - 2, 1)
            pe.wait_ge(act_x2, G + 1)
            for f in range(3):
                if f > 0:
                    pe.wait_ge(dve_out, TILES * (G - 2) + f)
                ffn1(rest_ps[f], f)
            ffn2(d_ps[1], 2, [(3 * (G - 1) + 1, range(4)), (3 * (G - 1) + 2, range(4, HC))])
            for f in range(3):
                pe.wait_ge(act_gh, 3 * (G - 1) + 2 + f + 1)
                for c in (2 * f, 2 * f + 1):
                    for t in range(2 if c < HC - 1 else 0):
                        high_product(v_ps[t], c, t)
            pe.wait_ge(dve_gl, 3 * G + 2)
            for t in range(2):
                for c in range(HC):
                    low_product(v_ps[t], c, t)
                high_product(v_ps[t], HC - 1, t).then_inc(pe_f2, 1)

        @block.scalar
        def _(act):
            act.dma_start(hcls[:], cls.partition_broadcast(P)).then_inc(cls_in, 16)
            act.dma_start(wqkv_raw[:], wqkv).then_inc(wqkv_in, 16)
            for dst, src in ((id_s[:], ident), (mask_s[:], hmask), (bqkv_s[:], bqkv),
                             (pbias_s[:], pbias.partition_broadcast(P)), (bout_s[:], bout.partition_broadcast(P)),
                             (bv_s[:], bv.partition_broadcast(P))):
                act.dma_start(dst, src).then_inc(small_in, 16)

            def exp(s):
                act.wait_ge(dve_sub, s + 1)
                if s >= 1:
                    act.wait_ge(pe_pt, s)
                act.activation(pexp[:], ssub[:], ACT.Exp, scale=SCALE).then_inc(act_exp, 1)

            def p_out(s):
                act.wait_ge(pe_pt, s + 1)
                act.activation(pT[:, s % 2].rearrange("p a b q -> p (a b q)"), attn_bank(s)[0:HK, :], ACT.Copy).then_inc(act_pt, 1)

            def c_out(s):
                g = s // STEPS
                act.wait_ge(pe_ct, s + 1)
                if s % STEPS == 0 and g >= 2:
                    act.wait_ge(pe_o, TILES * (g - 1))
                src = attn_bank(s)[0:EH, :].rearrange("p (h b q) -> p h b q", h=2, q=32)
                dst = cT[:, g % 2, :, (s % STEPS) * P:(s % STEPS + 1) * P].rearrange("p h (b q) -> p h b q", q=NP)
                act.activation(dst, src[:, :, :, 0:NP], ACT.Copy)
                act.activation(cTc[:, :, s * SB:(s + 1) * SB], src[:, :, :, NP], ACT.Copy).then_inc(act_ct, 1)

            def with_bias(f, m, src, dst):
                return act.activation(dst, src, ACT.Identity, bias=bqkv_s[:, 2 * f + m:2 * f + m + 1])

            def images(f, r, m):
                return (qT[:, r, m, 0:QT], kT[:, m, :])[f].rearrange("p (b t) -> p b t", t=NT)

            def qk_out(g, f):
                act.wait_ge(pe_qk, 2 * g + (1 if f == 1 else 2))
                if f == 0 and g >= 2:
                    act.wait_ge(pe_s, STEPS * (g - 1))
                if f == 1 and g >= 1:
                    act.wait_ge(dve_k, g)
                for m in range(2):
                    bank = half_bank(g, f, m)[0:EH, :]
                    last = with_bias(f, m, bank[:, 0:GT].rearrange("p (b t) -> p b t", t=NP),
                                     images(f, g % 2, m)[:, :, 0:NP])
                    if g == 0:
                        for r in range(2 if f == 0 else 1):
                            last = with_bias(f, m, bank[:, GT:GT + GB], images(f, r, m)[:, :, NP])
                last.then_inc(act_qk, 1)

            def turn_out(bank, xT, t):
                return act.activation(xT[:, :, t * P:(t + 1) * P],
                                      bank[:, 0:3 * P].rearrange("p (c t) -> p c t", c=3), ACT.Copy)

            def high(xs, xn, n, at=0):
                return act.activation(xs[:, at:at + n, 0, :], xn[:, at:at + n, :], ACT.Copy)

            splits = [0]

            def hidden(src, chunks, cols):
                splits[0] += 1
                n, k, w = splits[0], len(chunks), cols.stop - cols.start
                raw = gl_raw[:, n % 2, :]
                if n >= 3:
                    act.wait_ge(dve_gl, n - 2)
                for m, c in enumerate(chunks):
                    last = act.activation(raw[:, m * w:(m + 1) * w], src[:, m * w:(m + 1) * w], ACT.Gelu,
                                          bias=bin_s[:, c:c + 1])
                last.then_inc(act_g, 1)
                act.wait_ge(act_g, n)
                act.activation(gl[0][:, chunks[0]:chunks[0] + k, cols],
                               raw[:, 0:k * w].rearrange("p (c n) -> p c n", c=k), ACT.Copy).then_inc(act_gh, 1)

            def gelu(g, f):
                act.wait_ge(pe_f1, 3 * g + f + 1)
                if f == 0 and g >= 1:
                    act.wait_ge(pe_f2, TILES * g)
                hidden(ffn_bank(g, f), (2 * f, 2 * f + 1), slice(0, GT))

            act.wait_ge(small_in, 16 * 6)
            act.activation(id_r[:], id_s[:], ACT.Copy)
            act.wait_ge(dve_cls_xn, 1)
            high(xs1, xn1, 1).then_inc(act_cls_hi, 1)
            act.wait_ge(wqkv_in, 16)
            act.activation(wqkv_hi[:], wqkv_raw[:], ACT.Copy).then_inc(act_w, 1)
            act.wait_ge(pe_cls_t, 1)
            act.activation(xT1[:, :, GT:GT + CW], d_ps[0][:, 0:3 * P].rearrange("p (c t) -> p c t", c=3)[:, :, 0:CW],
                           ACT.Copy).then_inc(act_cls_x, 1)
            act.wait_ge(dve_init, 2)
            def turned_1(p):
                act.wait_ge(pe_t1, p + 1)
                if p >= 1:
                    act.wait_ge(pe_qk, 2 * p)
                    act.wait_ge(pe_v, p + 1)
                for t in range(TILES):
                    last = turn_out(turn_bank(p, t), xT1, t)
                last.then_inc(act_x1, 1)

            def high_1(a):
                act.wait_ge(dve_xn, a + 1)
                if a >= 1:
                    act.wait_ge(pe_t1, a)
                high(xs1, xn1, TILES).then_inc(act_hi1, 1)

            high_1(0)
            turned_1(0)
            high_1(1)
            act.wait_ge(win_in, 16)
            act.activation(win_hi[:], win_raw, ACT.Copy).then_inc(act_w, 1)
            qk_out(0, 1)
            for i in range(G):
                prj, emb = i + 1 < G, i + 2 < G
                p, a, d = i + 1, i + 2, i - 1
                s0, s1 = STEPS * i, STEPS * i + 1
                if prj:
                    turned_1(p)
                if i == 0:
                    qk_out(0, 0)
                    qk_out(p, 1)
                exp(s0)
                if i == 0:
                    p_out(s0)
                    qk_out(p, 0)
                    act.wait_ge(late_in, 16 * 3)
                    act.activation(w2_s[:, :, 0], w2_raw, ACT.Copy).then_inc(act_w, 1)
                    exp(s1)
                    high_1(a)
                    p_out(s1)
                    c_out(s0)
                    c_out(s1)
                    continue
                p_out(s0)
                if i == 1:
                    qk_out(p, 1)
                act.wait_ge(dve_xn2, d + 1)
                if d >= 1:
                    act.wait_ge(pe_t2, d)
                high(xs2, xn2, TILES).then_inc(act_hi2, 1)
                if i == G - 2:
                    qk_out(p, 1)
                exp(s1)
                if not emb:
                    c_out(s0)
                if i == 1:
                    c_out(s0)
                act.wait_ge(pe_t2, d + 1)
                if d >= 1:
                    act.wait_ge(pe_f1, 3 * d)
                turn_out(v_ps[0], xT2, 0)
                turn_out(v_ps[1], xT2, 1).then_inc(act_x2, 1)
                if emb and i >= 2:
                    c_out(s0)
                    qk_out(p, 1)
                if i == G - 2:
                    qk_out(p, 0)
                p_out(s1)
                if emb:
                    high_1(a)
                    qk_out(p, 0)
                if d == 0:
                    act.wait_ge(late_in, 16 * 3)
                gelu(d, 0)
                if i == G - 1:
                    act.wait_ge(dve_xn2, G)
                    high(xs2, xn2, 1, at=2).then_inc(act_hi2, 1)
                    c_out(s1)
                gelu(d, 1)
                if i < G - 1:
                    gelu(d, 2)
                    c_out(s1)

            act.wait_ge(pe_t2, G)
            turn_out(d_ps[0], xT2, 2).then_inc(act_x2, 1)
            gelu(G - 2, 2)
            act.wait_ge(dve_xn2, G + 1)
            act.wait_ge(pe_t2, G - 1)
            high(xs2, xn2, 2).then_inc(act_hi2, 1)
            for bank, part in ((v_ps[0], range(4)), (v_ps[1], range(4, HC))):
                act.wait_ge(pe_f1, 3 * (G - 1) + (1 if part[0] == 0 else 2))
                hidden(bank, part, slice(GT, GT + P))
            act.wait_ge(pe_t2, G + 1)
            act.wait_ge(pe_f1, 3 * (G - 1))
            turn_out(d_ps[0], xT2, 0)
            turn_out(s_ps, xT2, 1).then_inc(act_x2, 1)
            act.wait_ge(pe_f2, TILES * (G - 1))
            for f in range(3):
                act.wait_ge(pe_f1, 3 * (G - 1) + 2 + f + 1)
                hidden(rest_ps[f], (2 * f, 2 * f + 1), slice(0, GT))

        @block.vector
        def _(dve):
            linked = [0]

            def link(ins):
                linked[0] += 1
                ins.then_inc(dve_chain, 1)
                dve.wait_ge(dve_chain, linked[0])

            def stats(src, ln, n, at=0):
                for t in range(at, at + n):
                    link(dve.bn_stats(st[:, ln, t, :], src(t)))
                for t in range(at, at + n):
                    ins = dve.bn_aggr(mv[:, ln, t, :], st[:, ln, t, :])
                link(ins)
                dve.tensor_scalar(ve[:, ln, at:at + n], mv[:, ln, at:at + n, 1], EPS, None,
                                  ALU.add).then_inc(dve_ve, 1)

            def normalise(src, dst, ln, n, what, at=0):
                dve.wait_ge(pool_rstd, nth[what])
                for t in range(at, at + n):
                    ins = dve.tensor_scalar(dst[:, t, :], src(t), mv[:, ln, t, 0:1], rstd[:, ln, t:t + 1],
                                            ALU.subtract, ALU.mult)
                return ins

            def low(xs, xn, n, at=0):
                return dve.tensor_tensor(xs[:, at:at + n, 1, :], xn[:, at:at + n, :],
                                         xs[:, at:at + n, 0, :].bitcast(F32), ALU.subtract)

            def softmax_top(s):
                dve.wait_ge(pe_s, s + 1)
                sc = s_ps[:, 0:2 * HEADS * NT].rearrange("p (h k) -> p h k", k=NT)
                link(dve.tensor_reduce(smax[:], sc, AX.X, ALU.max))
                if s >= 1:
                    dve.wait_ge(act_exp, s)
                dve.tensor_tensor(ssub[:].rearrange("p a (h k) -> p (a h) k", k=NT), sc,
                                  smax[:].unsqueeze(2).to_broadcast([P, 2 * HEADS, NT]),
                                  ALU.subtract).then_inc(dve_sub, 1)

            def softmax_sum(s):
                dve.wait_ge(act_exp, s + 1)
                link(dve.tensor_reduce(ssum[:], pexp[:].rearrange("p a (h k) -> p (a h) k", k=NT), AX.X, ALU.add))
                dve.reciprocal(rinv[:], ssum[:]).then_inc(dve_chain, 1)
                linked[0] += 1
                return linked[0]

            def context(s, summed):
                dve.wait_ge(pe_pv, s + 1)
                dve.wait_ge(dve_chain, summed)
                if s >= 1:
                    dve.wait_ge(pe_ct, s)
                dve.tensor_tensor(cx.rearrange("p a (h d) -> p (a h) d", d=DK),
                                  attn_bank(s)[:, 0:2 * E].rearrange("p (h d) -> p h d", d=DK),
                                  rinv[:].unsqueeze(2).to_broadcast([P, 2 * HEADS, DK]),
                                  ALU.mult).then_inc(dve_cx, 1)

            def masks(g):
                dve.wait_ge(act_qk, 2 * g + 1)
                if g >= 1:
                    dve.wait_ge(pe_s, STEPS * g)
                for h in range(HH):
                    ins = dve.tensor_scalar(
                        kbd[:, :, :, h * NT:(h + 1) * NT].rearrange("p a b t -> p (a b) t"),
                        kT[:].rearrange("p a (b t) -> p (a b) t", t=NT), mask_s[:, h:h + 1], None, ALU.mult)
                ins.then_inc(dve_k, 1)

            def values(g):
                dve.wait_ge(pe_v, g + 2)
                if g >= 1:
                    dve.wait_ge(v_stored, 16 * g)
                dve.tensor_tensor(v_tok, qkv_bank(g, 2)[:, 0:TILES * E].rearrange("p (t e) -> p t e", e=E),
                                  bv_s[:].unsqueeze(1).to_broadcast([P, TILES, E]), ALU.add).then_inc(dve_val, 1)

            dve.memset(cT[:, 0].rearrange("p h t -> p (h t)"), 0.0).then_inc(dve_init, 1)
            dve.memset(mhalf[:], -0.5)
            for r in range(2):
                for m in range(2):
                    ins = dve.memset(qT[:, r, m, QT:QW], 0.0)
            ins.then_inc(dve_init, 1)
            dve.wait_ge(cls_in, 16)
            stats(lambda t: hcls[:], 0, 1)
            normalise(lambda t: hcls[:], xn1, 0, 1, ("cls", 0)).then_inc(dve_cls_xn, 1)
            dve.wait_ge(act_cls_hi, 1)
            low(xs1, xn1, 1).then_inc(dve_cls_lo, 1)
            dve.wait_ge(act_w, 1)
            dve.tensor_tensor(wqkv_lo[:], wqkv_raw[:, 0:2], wqkv_hi[:, 0:2].bitcast(F32),
                              ALU.subtract).then_inc(dve_w, 1)
            dve.wait_ge(small_in, 16 * 6)
            dve.wait_ge(pe_v, 1)
            dve.tensor_tensor(vcls[:], d_ps[2][0:CW, 0:E], bv_s[0:CW, :], ALU.add).then_inc(dve_cls_val, 1)
            for n in range(4):
                dve.wait_ge(pe_fold, n + 1)
                dve.tensor_copy(wf[:, n // 2].rearrange("p c e -> p (c e)")[:, (n % 2) * 288:(n % 2 + 1) * 288],
                                fold_ps[n][:, 0:288]).then_inc(dve_fold, 1)

            def embedded(a, t):
                dve.wait_ge(pe_embed, TILES * a + t + 1)
                if a >= 2 and t == 0:
                    dve.wait_ge(pool_hb, a - 1)
                dve.tensor_tensor(h_s[:, a % 2, t, :], embed_bank(a, t)[:, 0:E], pbias_s[:],
                                  ALU.add).then_inc(dve_h, 1)

            def norm_stats_1(a):
                dve.wait_ge(dve_h, TILES * (a + 1))
                stats(lambda t: h_s[:, a % 2, t, :], 0, TILES)

            def norm_1(a):
                if a >= 1:
                    dve.wait_ge(act_hi1, a)
                normalise(lambda t: h_s[:, a % 2, t, :], xn1, 0, TILES, ("ln1", a)).then_inc(dve_xn, 1)

            def low_1(a):
                dve.wait_ge(dve_xn, a + 1)
                dve.wait_ge(act_hi1, a + 1)
                low(xs1, xn1, TILES).then_inc(dve_lo, 1)

            def low_hidden(n, chunks, cols):
                k, w = len(chunks), cols.stop - cols.start
                dve.wait_ge(act_gh, n)
                at = slice(chunks[0], chunks[0] + k)
                dve.tensor_tensor(gl[1][:, at, cols], gl_raw[:, n % 2, 0:k * w].rearrange("p (c n) -> p c n", c=k),
                                  gl[0][:, at, cols].bitcast(F32), ALU.subtract).then_inc(dve_gl, 1)

            def low_gelu(g, f):
                low_hidden(3 * g + f + 1, (2 * f, 2 * f + 1), slice(0, GT))

            def output(dst, bank, res):
                link(dve.tensor_tensor(dst, bank[:, 0:E], res, ALU.add))
                dve.tensor_tensor(dst, bank[:, E:2 * E], dst, ALU.add).then_inc(dve_out, 1)

            def finished(e, t):
                if e >= 2 and t == 0:
                    dve.wait_ge(out_done[e % 2], 16 * (e // 2))
                dve.wait_ge(pe_f2, TILES * e + t + 1)
                output(os_[:, e % 2, t, :], d_ps[2 + t], h2[:, e % 2, t, :])

            for t in range(TILES):
                embedded(0, t)
            norm_stats_1(0)
            norm_1(0)
            low_1(0)
            for t in range(TILES):
                embedded(1, t)
            norm_stats_1(1)
            norm_1(1)
            embedded(2, 0)
            low_1(1)
            embedded(2, 1)
            values(0)
            masks(0)
            norm_stats_1(2)
            for i in range(G):
                prj, emb = i + 1 < G, i + 2 < G
                p, a, d = i + 1, i + 2, i - 1
                s0, s1 = STEPS * i, STEPS * i + 1
                if i == 0:
                    softmax_top(s0)
                    values(p)
                    norm_1(a)
                    summed = softmax_sum(s0)
                    softmax_top(s1)
                    embedded(a + 1, 0)
                    context(s0, summed)
                    masks(p)
                    summed = softmax_sum(s1)
                    low_1(a)
                    context(s1, summed)
                    continue
                if i == 1:
                    embedded(a, 1)
                softmax_top(s0)
                if i >= 2:
                    finished(i - 2, 0)
                if i >= 2:
                    summed = softmax_sum(s0)
                if 2 <= i < G - 1:
                    finished(i - 2, 1)
                dve.wait_ge(pool_hb, d + 1)
                for t in range(TILES):
                    dve.wait_ge(pe_o, TILES * d + t + 1)
                    dve.tensor_tensor(h2[:, d % 2, t, :], d_ps[t][:, 0:E], hb_s[:, d % 4, t, :],
                                      ALU.add).then_inc(dve_h2, 1)
                dve.wait_ge(dve_h2, TILES * (d + 1))
                stats(lambda t: h2[:, d % 2, t, :], 1, TILES)
                if i == 1:
                    summed = softmax_sum(s0)
                if v_early(p):
                    values(p)
                if d >= 1:
                    dve.wait_ge(act_hi2, d)
                normalise(lambda t: h2[:, d % 2, t, :], xn2, 1, TILES, ("ln2", d)).then_inc(dve_xn2, 1)
                dve.wait_ge(dve_xn2, d + 1)
                if emb and i >= 2:
                    embedded(a, 0)
                context(s0, summed)
                if i in (1, G - 1):
                    softmax_top(s1)
                dve.wait_ge(act_hi2, d + 1)
                low(xs2, xn2, TILES).then_inc(dve_lo2, 1)
                if i not in (1, G - 1):
                    softmax_top(s1)
                if emb:
                    if i >= 2:
                        embedded(a, 1)
                    norm_stats_1(a)
                if i == G - 2:
                    values(p)
                summed = softmax_sum(s1)
                if emb:
                    norm_1(a)
                if i == 1:
                    values(p)
                if prj:
                    masks(p)
                if i == G - 1:
                    finished(i - 2, 1)
                    dve.wait_ge(pe_o, TILES * i + 1)
                    dve.wait_ge(pool_hb, i + 1)
                    link(dve.tensor_tensor(h2[:, i % 2, 0, :], d_ps[0][:, 0:E], hb_s[:, i % 4, 0, :], ALU.add))
                    stats(lambda t: h2[:, i % 2, 0, :], 1, 1, at=2)
                context(s1, summed)
                if i == G - 1:
                    normalise(lambda t: h2[:, i % 2, 0, :], xn2, 1, 1, ("early", 0), at=2).then_inc(dve_xn2, 1)
                    dve.wait_ge(dve_xn2, G)
                    dve.wait_ge(act_hi2, G)
                    low(xs2, xn2, 1, at=2).then_inc(dve_lo2, 1)
                low_gelu(d, 0)
                if emb:
                    low_1(a)
                low_gelu(d, 1)
                if i < G - 1:
                    low_gelu(d, 2)

            d = G - 1
            last_h2 = [h2[:, d % 2, 1, :], h2c[:]]
            for t in range(2):
                dve.wait_ge(pe_o, TILES * d + t + 2)
                ins = dve.tensor_tensor(last_h2[t], (s_ps, a_ps)[t][:, 0:E], (hb_s[:, d % 4, 1, :], hbcls[:])[t],
                                        ALU.add)
            link(ins)
            stats(lambda t: last_h2[t], 1, 2)
            low_gelu(G - 2, 2)
            dve.wait_ge(act_hi2, G - 1)
            normalise(lambda t: last_h2[t], xn2, 1, 2, ("ln2", d)).then_inc(dve_xn2, 1)
            dve.wait_ge(dve_xn2, G + 1)
            dve.wait_ge(act_hi2, G + 1)
            low(xs2, xn2, 2).then_inc(dve_lo2, 1)
            finished(G - 2, 0)
            low_hidden(3 * (G - 1) + 1, range(4), slice(GT, GT + P))
            low_hidden(3 * (G - 1) + 2, range(4, HC), slice(GT, GT + P))
            finished(G - 2, 1)
            dve.wait_ge(out_done[d % 2], 16 * (d // 2))
            for f in range(3):
                low_hidden(3 * (G - 1) + 2 + f + 1, (2 * f, 2 * f + 1), slice(0, GT))
            dve.wait_ge(pe_f2, TILES * d + 1)
            output(os_[:, d % 2, 0, :], d_ps[1], h2[:, d % 2, 0, :])
            for t in range(2):
                dve.wait_ge(pe_f2, TILES * d + t + 2)
                output((os_[:, d % 2, 1, :], osc[:])[t], v_ps[t], last_h2[t])

        @block.gpsimd
        def _(pool):
            def inverse_root(ln, n, what, at=0):
                pool.wait_ge(dve_ve, nth[what])
                pool.tensor_tensor(rstd[:, ln, at:at + n], ve[:, ln, at:at + n], mhalf[:, 0:n],
                                   ALU.pow).then_inc(pool_rstd, 1)

            pool.wait_ge(dve_init, 2)
            inverse_root(0, 1, ("cls", 0))
            pool.memset(vbd[:].rearrange("p r b f e -> p (r b f e)"), 0.0).then_inc(pool_zero, 1)
            pool.wait_ge(small_in, 16 * 6)
            pool.wait_ge(cls_in, 16)
            pool.tensor_tensor(hbcls[:], hcls[:], bout_s[:], ALU.add)
            for i in ITER:
                a, d = i + 2, i - 1
                if d >= 0:
                    inverse_root(1, TILES, ("ln2", d))
                if i == G - 1:
                    inverse_root(1, 1, ("early", 0), at=2)
                if a < G:
                    inverse_root(0, TILES, ("ln1", a))
                    pool.tensor_tensor(hb_s[:, a % 4], h_s[:, a % 2], bout_s[:].unsqueeze(1).to_broadcast([P, TILES, E]),
                                       ALU.add).then_inc(pool_hb, 1)
                if i == 0:
                    pool.wait_ge(act_w, 3)
                    pool.tensor_tensor(w2_s[:, :, 1], w2_raw, w2_s[:, :, 0].bitcast(F32),
                                       ALU.subtract).then_inc(pool_w, 1)
                if i == -1:
                    pool.wait_ge(act_w, 2)
                    pool.tensor_tensor(win_lo[:], win_raw[:, 0:2], win_hi[:, 0:2].bitcast(F32),
                                       ALU.subtract).then_inc(pool_w, 1)


def kernel(x, cls_tok, L0_tok_proj_weight, L0_tok_proj_bias, L0_tok_pinv, L0_attn_w_qkv, L0_attn_b_qkv,
           L0_attn_w_out, L0_attn_b_out, L0_ffn_in_weight, L0_ffn_in_bias, L0_ffn_out_weight):
    import numpy as np
    import concourse.bacc as bacc
    from concourse.bass_utils import run_bass_kernel_spmd

    def lay(a):
        return np.ascontiguousarray(a)

    def chunks(w):
        return np.concatenate([w, w], axis=0).reshape(3, P, -1).transpose(1, 0, 2)

    xp = np.asarray(x).reshape(G, GB, C, 4, 16, 4, 16).transpose(0, 2, 4, 6, 1, 3, 5)
    xp = xp.reshape(G, XC, P, GT).transpose(0, 2, 1, 3)
    wt = np.asarray(L0_tok_proj_weight).reshape(E, C, OC, P).transpose(3, 2, 1, 0).reshape(P, OC, C * E)
    pinvt = np.asarray(L0_tok_pinv).reshape(PIX, OC, P).transpose(2, 1, 0)
    arrays = {
        "xt": lay(xp), "wt": lay(wt), "pinvt": lay(pinvt),
        "pbias": lay(L0_tok_proj_bias), "cls": lay(np.asarray(cls_tok).reshape(E)),
        "wqkv": lay(chunks(np.asarray(L0_attn_w_qkv))),
        "bqkv": lay(np.asarray(L0_attn_b_qkv).reshape(6, EH).T),
        "bv": lay(np.asarray(L0_attn_b_qkv)[2 * E:]),
        "wout": lay(np.asarray(L0_attn_w_out).reshape(2, EH, E).transpose(1, 0, 2)),
        "bout": lay(L0_attn_b_out),
        "win": lay(chunks(np.asarray(L0_ffn_in_weight).T)),
        "bin_": lay(np.asarray(L0_ffn_in_bias).reshape(HC, P).T),
        "w2": lay(np.asarray(L0_ffn_out_weight).reshape(HC, P, E).transpose(1, 0, 2)),
        "ident": np.eye(P, dtype=np.float32),
        "hmask": np.repeat(np.eye(HH, dtype=np.float32), DK, axis=0),
    }
    nc = bacc.Bacc("TRN2", target_bir_lowering=False, num_devices=1)
    args = [nc.dram_tensor(n, a.shape, F32, kind="ExternalInput").ap() for n, a in arrays.items()]
    v_dram = nc.dram_tensor("v_dram", [G, GT, E], F32, kind="Internal").ap()
    vcls_dram = nc.dram_tensor("vcls_dram", [CW, E], F32, kind="Internal").ap()
    out_p = nc.dram_tensor("out_p", [G, P, TILES, E], F32, kind="ExternalOutput").ap()
    out_c = nc.dram_tensor("out_c", [B, E], F32, kind="ExternalOutput").ap()
    vit_tower(nc, *args, v_dram, vcls_dram, out_p, out_c)
    r = run_bass_kernel_spmd(nc, [arrays], core_ids=[0]).results[0]
    patches = np.asarray(r["out_p"]).transpose(0, 2, 1, 3).reshape(B, NP, E)
    return np.concatenate([np.asarray(r["out_c"]).reshape(B, 1, E), patches], axis=1)
```
